# Optimizing a Trainium2 kernel written in Bass

```python
import numpy as np
import jax
import jax.numpy as jnp

def _softmax(x, axis=-1):
    return jax.nn.softmax(x, axis=axis)

def _gelu(x):
    return jax.nn.gelu(x, approximate=True)

def _silu(x):
    return jax.nn.silu(x)

def _sigmoid(x):
    return jax.nn.sigmoid(x)

def _layernorm(x, axis=-1, eps=1e-05):
    m = jnp.mean(x, axis=axis, keepdims=True)
    v = jnp.var(x, axis=axis, keepdims=True)
    return (x - m) / jnp.sqrt(v + eps)

def _scatter_add(tgt, idx, src, axis=0):
    return tgt.at[idx].add(src)

def _segment_sum(src, seg, n):
    return jax.ops.segment_sum(src, seg, n)
kernel_name = 'mk_recurrent_d1_jaxref_r8_bcf1b4'

def setup_inputs(seed: int=0):
    np.random.seed(seed)
    _w = jnp.asarray

    def _L0_attn_setup():
        import jax, jax.numpy as jnp
        import numpy as np
        import math
        B, T, D = (4, 512, 128)
        H, DK, DV, C = (8, 128, 128, 64)

        def _rms_norm(x, eps=1e-06):
            return x * jax.lax.rsqrt(jnp.mean(x * x, axis=-1, keepdims=True) + eps)
        key = jax.random.key(seed)
        ks = jax.random.split(key, 7)
        s = 0.02
        return {'x': jax.random.normal(ks[0], (B, T, D), jnp.float32), 'Wq': jax.random.normal(ks[1], (H * DK, D), jnp.float32) * s, 'Wk': jax.random.normal(ks[2], (H * DK, D), jnp.float32) * s, 'Wv': jax.random.normal(ks[3], (H * DV, D), jnp.float32) * s, 'Wg': jax.random.normal(ks[4], (H, D), jnp.float32) * s, 'bg': jnp.full((H,), 3.0, jnp.float32), 'Wo': jax.random.normal(ks[5], (D, H * DV), jnp.float32) * s, 'qk_gain': jnp.asarray(4.0, jnp.float32)}
    _L0_attn_in = _L0_attn_setup()

    def _L0_ffn_setup():
        import jax, jax.numpy as jnp
        import numpy as np
        DIM = 128

        def _reference_tuple_inner(x, W_r, W_k, W_v, mu_r, mu_k):
            B, T, C = x.shape
            x_prev = jnp.concatenate([jnp.zeros((B, 1, C), x.dtype), x[:, :-1, :]], axis=1)
            xr = mu_r * x + (1.0 - mu_r) * x_prev
            xk = mu_k * x + (1.0 - mu_k) * x_prev
            r = jax.nn.sigmoid(jnp.einsum('btc,dc->btd', xr, W_r))
            k = jnp.einsum('btc,dc->btd', xk, W_k)
            k_act = jnp.square(jax.nn.relu(k))
            out = r * jnp.einsum('btc,dc->btd', k_act, W_v)
            new_state = x[:, -1, :]
            return (out, new_state)
        key = jax.random.key(seed)
        ks = jax.random.split(key, 6)
        B, T, C = (8, 256, DIM)
        x = jax.random.normal(ks[0], (B, T, C), dtype=jnp.float32)
        s = 1.0 / np.sqrt(C)
        W_r = jax.random.uniform(ks[1], (C, C), jnp.float32, -s, s)
        W_k = jax.random.uniform(ks[2], (C, C), jnp.float32, -s, s)
        W_v = jax.random.uniform(ks[3], (C, C), jnp.float32, -s, s)
        mu_r = jax.random.uniform(ks[4], (C,), jnp.float32)
        mu_k = jax.random.uniform(ks[5], (C,), jnp.float32)
        return {'x': x, 'W_r': W_r, 'W_k': W_k, 'W_v': W_v, 'mu_r': mu_r, 'mu_k': mu_k}
    _L0_ffn_in = _L0_ffn_setup()
    _d = {'L0_attn_x': _L0_attn_in['x'], 'L0_attn_Wq': _L0_attn_in['Wq'], 'L0_attn_Wk': _L0_attn_in['Wk'], 'L0_attn_Wv': _L0_attn_in['Wv'], 'L0_attn_Wg': _L0_attn_in['Wg'], 'L0_attn_bg': _L0_attn_in['bg'], 'L0_attn_Wo': _L0_attn_in['Wo'], 'L0_attn_qk_gain': _L0_attn_in['qk_gain'], 'L0_ffn_W_r': _L0_ffn_in['W_r'], 'L0_ffn_W_k': _L0_ffn_in['W_k'], 'L0_ffn_W_v': _L0_ffn_in['W_v'], 'L0_ffn_mu_r': _L0_ffn_in['mu_r'], 'L0_ffn_mu_k': _L0_ffn_in['mu_k']}
    _x0 = _d['L0_attn_x']
    _d['L0_attn_x'] = jax.random.normal(jax.random.fold_in(jax.random.key(seed), 1), (16, 512, 128), dtype=_x0.dtype)
    del _x0
    return _d

def reference(L0_attn_x, L0_attn_Wq, L0_attn_Wk, L0_attn_Wv, L0_attn_Wg, L0_attn_bg, L0_attn_Wo, L0_attn_qk_gain, L0_ffn_W_r, L0_ffn_W_k, L0_ffn_W_v, L0_ffn_mu_r, L0_ffn_mu_k):

    def _L0_attn_ref(x, Wq, Wk, Wv, Wg, bg, Wo, qk_gain):
        import jax, jax.numpy as jnp
        import numpy as np
        import math
        B, T, D = (4, 512, 128)
        H, DK, DV, C = (8, 128, 128, 64)

        def _rms_norm(x, eps=1e-06):
            return x * jax.lax.rsqrt(jnp.mean(x * x, axis=-1, keepdims=True) + eps)
        Bs, Ts, Ds = x.shape
        pad = (C - Ts % C) % C
        if pad:
            x = jnp.pad(x, ((0, 0), (0, pad), (0, 0)))
        Tp = x.shape[1]
        n = Tp // C
        q = (x @ Wq.T).reshape(Bs, Tp, H, DK).transpose(0, 2, 1, 3)
        k = (x @ Wk.T).reshape(Bs, Tp, H, DK).transpose(0, 2, 1, 3)
        v = (x @ Wv.T).reshape(Bs, Tp, H, DV).transpose(0, 2, 1, 3)
        g = jax.nn.sigmoid(x @ Wg.T + bg).transpose(0, 2, 1)
        q = _rms_norm(q) * qk_gain
        k = _rms_norm(k)
        q = q.reshape(Bs, H, n, C, DK)
        k = k.reshape(Bs, H, n, C, DK)
        v = v.reshape(Bs, H, n, C, DV)
        g = g.reshape(Bs, H, n, C)
        mask = jnp.tril(jnp.ones((C, C), bool))
        scores = jnp.einsum('bhntd,bhnsd->bhnts', q, k) / math.sqrt(DK)
        scores = jnp.where(mask, scores, -jnp.inf)
        attn = jax.nn.softmax(scores, axis=-1)
        y_in = jnp.einsum('bhnts,bhnsd->bhntd', attn, v)
        kv = jnp.einsum('bhntd,bhnte->bhnde', k, v)
        gamma = jnp.exp(jnp.sum(jnp.log(g), axis=-1))
        qs = jnp.moveaxis(q, 2, 0)
        kvs = jnp.moveaxis(kv, 2, 0)
        gs = jnp.moveaxis(gamma, 2, 0)

        def step(state, inp):
            qn, kvn, gn = inp
            yc = jnp.einsum('bhtd,bhde->bhte', qn, state)
            new_state = state * gn[:, :, None, None] + kvn
            return (new_state, yc)
        state0 = jnp.zeros((Bs, H, DK, DV), x.dtype)
        _, ycs = jax.lax.scan(step, state0, (qs, kvs, gs))
        y_cross = jnp.moveaxis(ycs, 0, 2)
        y = (y_in + y_cross).reshape(Bs, H, Tp, DV).transpose(0, 2, 1, 3).reshape(Bs, Tp, H * DV)
        y = y @ Wo.T
        if pad:
            y = y[:, :Ts, :]
        return y

    def _L0_ffn_ref(x, W_r, W_k, W_v, mu_r, mu_k):
        import jax, jax.numpy as jnp
        import numpy as np
        DIM = 128

        def _reference_tuple_inner(x, W_r, W_k, W_v, mu_r, mu_k):
            B, T, C = x.shape
            x_prev = jnp.concatenate([jnp.zeros((B, 1, C), x.dtype), x[:, :-1, :]], axis=1)
            xr = mu_r * x + (1.0 - mu_r) * x_prev
            xk = mu_k * x + (1.0 - mu_k) * x_prev
            r = jax.nn.sigmoid(jnp.einsum('btc,dc->btd', xr, W_r))
            k = jnp.einsum('btc,dc->btd', xk, W_k)
            k_act = jnp.square(jax.nn.relu(k))
            out = r * jnp.einsum('btc,dc->btd', k_act, W_v)
            new_state = x[:, -1, :]
            return (out, new_state)
        return _reference_tuple_inner(x, W_r, W_k, W_v, mu_r, mu_k)[0]
    x = L0_attn_x
    xn = _layernorm(x, axis=-1)
    s = _L0_attn_ref(xn, L0_attn_Wq, L0_attn_Wk, L0_attn_Wv, L0_attn_Wg, L0_attn_bg, L0_attn_Wo, L0_attn_qk_gain)
    g = _silu(_L0_ffn_ref(xn, L0_ffn_W_r, L0_ffn_W_k, L0_ffn_W_v, L0_ffn_mu_r, L0_ffn_mu_k))
    x = x + s * g
    return x

_drawn_inputs = setup_inputs


def setup_inputs(seed=0):
    import zlib

    import numpy as np

    out = dict(_drawn_inputs(seed))
    spreads = {'L0_attn_bg': (3.0, 0.6)}
    factors = {'L0_attn_Wg': 42.917}
    for name, (base, spread) in spreads.items():
        noise = np.random.default_rng([zlib.crc32(name.encode()), seed]).standard_normal(out[name].shape)
        drawn = base * np.exp(spread * noise) if base else spread * noise
        out[name] = jnp.asarray(drawn.astype(out[name].dtype))
    for name, factor in factors.items():
        out[name] = (out[name] * factor).astype(out[name].dtype)
    return out
```

```python
from contextlib import ExitStack

import numpy as np
import concourse.bass as bass
from concourse import mybir

F32 = mybir.dt.float32
F32R = mybir.dt.float32r
BF16 = mybir.dt.bfloat16
ALU = mybir.AluOpType
ACT = mybir.ActivationFunctionType
AX = mybir.AxisListType

P = 128
CH = 64
BANK = 512
MASKED = -1.0e30
LN_EPS = 1.0e-5
RMS_EPS = 1.0e-6


def build(nc, x, Wq, Wk, Wv, Wg, bg, Wo, gain, Wr, Wkf, Wvf, mu_r, mu_k, out):
    NSEQ, T, D = x.shape
    H = Wg.shape[0]
    DK = Wq.shape[0] // H
    NT = T // P
    HW = H * D
    HB = BANK // D
    assert D == P and DK == P and T == BANK and H == 2 * HB and NT == 4 and NSEQ % 2 == 0
    SCALE = 1.0 / float(np.sqrt(DK))
    NR = 2 * H

    with ExitStack() as ctx:
        def sb(name, shape, dt=F32):
            return ctx.enter_context(nc.sbuf_tensor(name, shape, dt))

        def pair(name, shape, dt=F32):
            return [sb(f"{name}{i}", shape, dt) for i in range(2)]

        def bank(name, n=1):
            return ctx.enter_context(nc.psum_tensor(name, [P, n * BANK], F32))

        def sem(name):
            return ctx.enter_context(nc.semaphore(name))

        wqk_in = sb("wqk_in", [P, 2 * H, D])
        wq_in, wk_in = wqk_in[:, 0:H, :], wqk_in[:, H:2 * H, :]
        wv_in = sb("wv_in", [P, H, D])
        wo_in = sb("wo_in", [P, HW])
        wg_in = sb("wg_in", [H, D])
        ffn_in = sb("ffn_in", [P, 3, D])
        bg_all = sb("bg_all", [P, H])
        gain_all = sb("gain_all", [P, 1])
        mu = sb("mu", [P, 2])
        one_minus_mu = sb("one_minus_mu", [P, 2])
        eps = sb("eps", [P, 2])
        scratch = sb("scratch", [P, 1])
        mask = sb("mask", [P, CH])
        ident = sb("ident", [P, P])
        ident16 = sb("ident16", [P, P], BF16)
        pick = sb("pick", [P, NR, P], BF16)
        span = sb("span", [P, 3, P])
        woT = sb("woT", [P, H, D])
        small_wT = sb("small_wT", [P, 3 * D + H])
        w_hi = sb("w_hi", [P, 3 * HW], F32R)
        w_lo = sb("w_lo", [P, 3 * HW], F32R)
        a_hi = sb("a_hi", [P, HW], F32R)
        a_lo = sb("a_lo", [P, HW], F32R)
        xs = pair("xs", [P, NT, D])
        stats = sb("stats", [P, NT, 6])
        mean_var = sb("mean_var", [P, NT, 2])
        ln_var = sb("ln_var", [P, NT])
        rstd = sb("rstd", [P, NT])
        xn = pair("xn", [P, NT, D])
        xT = pair("xT", [P, 1 + T])
        xT_hi = pair("xT_hi", [P, T], F32R)
        xT_lo = pair("xT_lo", [P, T], F32R)
        p_raw = pair("p_raw", [P, H, T])
        mix_r = sb("mix_r", [P, T])
        mix_k = sb("mix_k", [P, T])
        xr = sb("xr", [P, T])
        xk = sb("xk", [P, T])
        r_exp = sb("r_exp", [P, T])
        r_sig = sb("r_sig", [P, T])
        k_relu = sb("k_relu", [P, T])
        k_act = sb("k_act", [P, T])
        ffn = sb("ffn", [P, T])
        f_exp = sb("f_exp", [P, T])
        gT = pair("gT", [P, T])
        zb = sb("zb", [P, NT, H])
        z_neg = sb("z_neg", [P, NT, H])
        z_l1p = sb("z_l1p", [P, NT, H])
        log_g = sb("log_g", [P, NT, H])
        decay = pair("decay", [P, 2, NT, H])
        q_decay = pair("q_decay", [P, NT, H, 2])
        sgT = sb("sgT", [P, T])
        y = sb("y", [P, NT, D])
        squared = wqk_in
        ssq = pair("ssq", [P, NR])
        ln_ms = sb("ln_ms", [P, NR])
        rms = pair("rms", [P, NR])
        res1 = sb("res1", [P, NR])
        res2 = sb("res2", [P, NR])
        parts = sb("parts", [P, P], BF16)
        partsT = pair("partsT", [P, P], BF16)
        vp = pair("vp", [P, HW])
        v_scale = sb("v_scale", [P, H])
        v_scaled = sb("v_scaled", [P, HW])
        k_rms = pair("k_rms", [P, HW])
        p_q = pair("p_q", [P, H, P])
        p_dec = sb("p_dec", [P, H, P])
        own = pair("own", [P, H, CH])
        top = sb("top", [P, H])
        total = sb("total", [P, H])
        inv_total = pair("inv_total", [P, H])
        att = pair("att", [P, H, P])
        attT = pair("attT", [P, H, P])
        state = sb("state", [P, H, D])

        PJ = [bank("PJ0"), bank("PJ1")]
        SC = bank("SC", 2)
        BK = [bank("BK0"), bank("BK1")]
        OUT = bank("OUT")
        MI = bank("MI")
        SCh = SC[:, :].rearrange("p (h s) -> p h s", h=H)
        MI16 = MI[:, :].bitcast(BF16)

        weights_in = sem("weights_in")
        x_in = [sem("x_in0"), sem("x_in1")]
        residual_in = sem("residual_in")
        y_out = sem("y_out")
        zeroed = sem("zeroed")
        consts_ready = sem("consts_ready")
        pick_ready = sem("pick_ready")
        small_ready = sem("small_ready")
        setup_filled = sem("setup_filled")
        setup_hi = sem("setup_hi")
        setup_read = sem("setup_read")
        stats_done = sem("stats_done")
        var_ready = sem("var_ready")
        lnvar_done = sem("lnvar_done")
        rstd_ready = sem("rstd_ready")
        xn_ready = sem("xn_ready")
        xT_filled = sem("xT_filled")
        xT_ready = sem("xT_ready")
        xhi_ready = sem("xhi_ready")
        xlo_ready = sem("xlo_ready")
        z_filled = sem("z_filled")
        zb_done = sem("zb_done")
        zneg_ready = sem("zneg_ready")
        zexp_done = sem("zexp_done")
        zl1p_ready = sem("zl1p_ready")
        logg_ready = sem("logg_ready")
        gates_filled = sem("gates_filled")
        decay_ready = sem("decay_ready")
        mix_ready = sem("mix_ready")
        xrk_ready = sem("xrk_ready")
        r_filled = sem("r_filled")
        rexp_ready = sem("rexp_ready")
        k_filled = sem("k_filled")
        krelu_ready = sem("krelu_ready")
        kact_ready = sem("kact_ready")
        rone_done = sem("rone_done")
        rsig_done = sem("rsig_done")
        v_filled = sem("v_filled")
        ffn_ready = sem("ffn_ready")
        fexp_ready = sem("fexp_ready")
        fone_done = sem("fone_done")
        fsig_done = sem("fsig_done")
        gT_ready = sem("gT_ready")
        proj_filled = sem("proj_filled")
        proj_read = sem("proj_read")
        lnms_done = sem("lnms_done")
        rms_ready = sem("rms_ready")
        gained = sem("gained")
        split_step = sem("split_step")
        parts_ready = sem("parts_ready")
        partsT_filled = sem("partsT_filled")
        partsT_ready = sem("partsT_ready")
        krms_filled = sem("krms_filled")
        krms_ready = sem("krms_ready")
        qrms_filled = sem("qrms_filled")
        pq_ready = sem("pq_ready")
        vscale_done = sem("vscale_done")
        vscaled_ready = sem("vscaled_ready")
        pdec_ready = sem("pdec_ready")
        scores_filled = sem("scores_filled")
        own_ready = sem("own_ready")
        mask_ready = sem("mask_ready")
        top_done = sem("top_done")
        shifted_ready = sem("shifted_ready")
        exp_ready = sem("exp_ready")
        total_done = sem("total_done")
        inv_ready = sem("inv_ready")
        att_a_ready = sem("att_a_ready")
        att_b_ready = sem("att_b_ready")
        attT_filled = sem("attT_filled")
        attT_ready = sem("attT_ready")
        cross_done = sem("cross_done")
        av_done = sem("av_done")
        incr_filled = sem("incr_filled")
        state_ready = sem("state_ready")
        sg_ready = sem("sg_ready")
        outT_filled = sem("outT_filled")
        y_ready = sem("y_ready")

        block = ctx.enter_context(nc.Block())

        def need(eng, s, n):
            if not (isinstance(n, int) and n <= 0):
                eng.wait_ge(s, n)

        def job(s, j, k):
            return 2 * HB + 6 + s * 32 + (0, 6, 12, 22)[j] + k

        def tile_job(s, j, k):
            if j > 0:
                return job(s, j - 1, k)
            if isinstance(s, int) and s == 0:
                return 2 * HB + k
            return job(s - 1, NT - 1, k)

        def p_job(s, h):
            if isinstance(s, int) and s == 0:
                return h
            return job(s - 1, 2 + h // HB, 6 + h % HB)

        def sequences(eng, run):
            run(0, 0, False)
            run(1, 1, False)
            with eng.Fori(1, NSEQ // 2 - 1) as i:
                run(i * 2, 0, False)
                run(i * 2 + 1, 1, False)
            run(NSEQ - 2, 0, False)
            run(NSEQ - 1, 1, True)

        SPLIT_JOBS = (0, 1, 2, 3, 7, 8, 9, 10)

        def split_dst(n, hi):
            cols = {0: 0, 1: BANK, 2: HW, 3: HW + BANK, 9: 2 * HW, 10: 2 * HW + BANK}
            if n in cols:
                t, c = (w_hi if hi else w_lo), cols[n]
            else:
                t, c = (a_hi if hi else a_lo), (n - 7) * BANK
            return t[:, c:c + BANK]

        @block.sync
        def _(sp):
            sp.dma_start(xs[0][:, :, :], x[0].rearrange("(j p) d -> p j d", p=P)).then_inc(x_in[0], 16)
            sp.dma_start(wq_in, Wq.rearrange("(h e) c -> e h c", h=H)).then_inc(weights_in, 16)
            sp.dma_start(wk_in, Wk.rearrange("(h e) c -> e h c", h=H)).then_inc(weights_in, 16)
            sp.dma_start(wv_in[:, :, :], Wv.rearrange("(h e) c -> e h c", h=H)).then_inc(weights_in, 16)
            sp.dma_start(wo_in[:, :], Wo).then_inc(weights_in, 16)
            sp.dma_start(wg_in[:, :], Wg).then_inc(weights_in, 16)
            for n, w in enumerate((Wr, Wkf, Wvf)):
                sp.dma_start(ffn_in[:, n, :], w).then_inc(weights_in, 16)
            sp.dma_start(bg_all[:, :], bg.partition_broadcast(P)).then_inc(weights_in, 16)
            sp.dma_start(gain_all[:, :], gain.partition_broadcast(P)).then_inc(weights_in, 16)
            sp.dma_start(mu[:, 0:1], mu_r.rearrange("(p o) -> p o", o=1)).then_inc(weights_in, 16)
            sp.dma_start(mu[:, 1:2], mu_k.rearrange("(p o) -> p o", o=1)).then_inc(weights_in, 16)
            sp.dma_start(xs[1][:, :, :], x[1].rearrange("(j p) d -> p j d", p=P)).then_inc(x_in[1], 16)

            def run(s, par, last):
                known = isinstance(s, int)
                if not (known and s + 2 >= NSEQ):
                    sp.wait_ge(xn_ready, s + 1)
                    sp.dma_start(xs[par][:, :, :], x[s + 2].rearrange("(j p) d -> p j d", p=P))\
                        .then_inc(x_in[par], 16)
                if not (known and s == 0):
                    sp.wait_ge(y_ready, s)
                    sp.dma_start(out[s - 1].rearrange("(j p) d -> p j d", p=P), y[:, :, :]).then_inc(y_out, 16)
                    sp.wait_ge(y_out, s * 16)
                sp.dma_start(y[:, :, :], x[s].rearrange("(j p) d -> p j d", p=P)).then_inc(residual_in, 16)

            sequences(sp, run)
            sp.wait_ge(y_ready, NSEQ)
            sp.dma_start(out[NSEQ - 1].rearrange("(j p) d -> p j d", p=P), y[:, :, :]).then_inc(y_out, 16)
            sp.wait_ge(y_out, 16 * NSEQ)

        NWEIGHTS = 16 * 12

        @block.tensor
        def _(pe):
            pe.wait_ge(weights_in, NWEIGHTS)
            pe.wait_ge(consts_ready, 1)
            pe.wait_ge(pick_ready, 8)
            for n in range(11):
                need(pe, setup_read, n - 1)
                pb = PJ[n % 2]
                if n < 4:
                    w = (wq_in, wk_in)[n // 2]
                    for i in range(HB):
                        last = pe.transpose(pb[:, i * D:(i + 1) * D], w[:, (n % 2) * HB + i, :], ident[:, :])
                elif n < 6:
                    for i in range(HB):
                        h = (n - 4) * HB + i
                        last = pe.transpose(pb[:, i * D:(i + 1) * D], wo_in[:, h * D:(h + 1) * D], ident[:, :])
                elif n == 6:
                    for i in range(3):
                        pe.transpose(pb[:, i * D:(i + 1) * D], ffn_in[:, i, :], ident[:, :])
                    last = pe.transpose(pb[:, 3 * D:3 * D + H], wg_in[:, :], ident[0:H, 0:H])
                elif n < 9:
                    for i in range(HB):
                        h = (n - 7) * HB + i
                        last = pe.matmul(pb[:, i * D:(i + 1) * D], wq_in[:, h, :], wk_in[:, h, :],
                                         start=True, stop=True)
                else:
                    for i in range(HB):
                        h = (n - 9) * HB + i
                        last = pe.matmul(pb[:, i * D:(i + 1) * D], wv_in[:, h, :], woT[:, h, :],
                                         start=True, stop=True)
                last.then_inc(setup_filled, 1)

            def xT_stage(s, par):
                pe.wait_ge(xn_ready, s + 1)
                for j in range(NT):
                    last = pe.transpose(MI[:, j * P:(j + 1) * P], xn[par][:, j, :], ident[:, :])
                last.then_inc(xT_filled, 1)

            def z_stage(s, par):
                pe.wait_ge(xhi_ready, s + 1)
                for j in range(NT):
                    last = pe.matmul(MI[:, j * H:(j + 1) * H], xT[par][:, 1 + j * P:1 + (j + 1) * P],
                                     small_wT[:, 3 * D:3 * D + H], start=True, stop=True)
                last.then_inc(z_filled, 1)

            def gate_stage(s):
                pe.wait_ge(logg_ready, s + 1)
                for kind in range(3):
                    last = pe.matmul(MI[:, kind * NT * H:(kind + 1) * NT * H], span[:, kind, :],
                                     log_g[:, :, :].rearrange("p j h -> p (j h)"), start=True, stop=True)
                last.then_inc(gates_filled, 1)

            def r_stage(s):
                pe.wait_ge(decay_ready, s + 1)
                pe.wait_ge(xrk_ready, s + 1)
                pe.matmul(MI[:, :], small_wT[:, 0:D], xr[:, :], start=True, stop=True).then_inc(r_filled, 1)

            def k_stage(s):
                pe.wait_ge(rexp_ready, s + 1)
                pe.matmul(MI[:, :], small_wT[:, D:2 * D], xk[:, :], start=True, stop=True).then_inc(k_filled, 1)

            def v_stage(s):
                pe.wait_ge(kact_ready, s + 1)
                pe.wait_ge(partsT_ready, s * NT + 2)
                pe.matmul(MI[:, :], small_wT[:, 2 * D:3 * D], k_act[:, :], start=True, stop=True)\
                    .then_inc(v_filled, 1)

            def product(n, pb, hi_lo_pairs):
                need(pe, proj_read, n - 1)
                for i, (lhsT, rhs) in enumerate(hi_lo_pairs):
                    last = pe.matmul(pb[:, :], lhsT, rhs, start=(i == 0), stop=(i == len(hi_lo_pairs) - 1))
                last.then_inc(proj_filled, 1)

            def p_stage(s, par, hs, first_job):
                pe.wait_ge(xlo_ready, s + 1)
                for i, h in enumerate(hs):
                    cols = slice(h * D, (h + 1) * D)
                    product(first_job + i, PJ[h % 2], [(a_hi[:, cols], xT_hi[par][:, :]), (a_hi[:, cols], xT_lo[par][:, :]),
                                            (a_lo[:, cols], xT_hi[par][:, :])])

            def project(par, j, first_job, ks):
                t = slice(j * P, (j + 1) * P)
                for k in ks:
                    cols = slice(k * BANK, (k + 1) * BANK)
                    product(first_job + k, PJ[k % 2], [(xT_hi[par][:, t], w_hi[:, cols]), (xT_hi[par][:, t], w_lo[:, cols]),
                                            (xT_lo[par][:, t], w_hi[:, cols])])

            def spread(dst, j0, b):
                for i in range(HB):
                    last = pe.matmul(dst[:, i * P:(i + 1) * P], pick[:, j0 + i, :], partsT[b % 2][:, :],
                                     start=True, stop=True)
                return last

            def turn(b, g):
                pe.wait_ge(att_a_ready, g + 1)
                pe.wait_ge(att_b_ready, g + 1)
                for half in range(2):
                    for h in range(half * HB, (half + 1) * HB):
                        last = pe.transpose(SC[:, h * P:(h + 1) * P], att[b][:, h, :], ident[:, :])
                    last.then_inc(attT_filled, 1)

            def attend(s, par, j):
                g = s * NT + j
                pe.wait_ge(proj_read, tile_job(s, j, 5) + 1)
                if j == 0:
                    need(pe, y_ready, s)
                for h in range(H):
                    if h % HB == 0:
                        pe.wait_ge(attT_ready, g * 2 + 1 + h // HB)
                    last = pe.matmul(OUT[:, j * P:(j + 1) * P], vp[j % 2][:, h * D:(h + 1) * D],
                                     attT[j % 2][:, h, :], start=(j == 0 and h == 0), stop=(h == H - 1))
                last.then_inc(av_done, 1)

            def finish(s):
                pe.wait_ge(sg_ready, s + 1)
                for j in range(NT):
                    last = pe.transpose(OUT[:, j * P:(j + 1) * P], sgT[:, j * P:(j + 1) * P], ident[:, :])
                last.then_inc(outT_filled, 1)

            pe.wait_ge(setup_read, 11)
            xT_stage(0, 0)
            z_stage(0, 0)
            gate_stage(0)
            r_stage(0)
            k_stage(0)
            p_stage(0, 0, range(H), 0)
            project(0, 0, 2 * HB, range(6))

            def run(s, par, last_s):
                for j in range(NT):
                    g = s * NT + j
                    nxt = not (last_s and j == NT - 1)
                    np_, nj = (par, j + 1) if j < NT - 1 else (1 - par, 0)
                    if nxt:
                        if j == NT - 1:
                            pe.wait_ge(xlo_ready, s + 2)
                        project(np_, nj, job(s, j, 0), (0,))
                    pe.wait_ge(parts_ready, g + 1)
                    if j == 0:
                        pe.wait_ge(krelu_ready, s + 1)
                        need(pe, partsT_ready, g)
                    elif j == 2:
                        if last_s:
                            pe.wait_ge(ffn_ready, s + 1)
                        else:
                            pe.wait_ge(xhi_ready, s + 2)
                    elif j == 3 and not last_s:
                        pe.wait_ge(krelu_ready, s + 2)
                    else:
                        pe.wait_ge(partsT_ready, g)
                    pe.transpose(MI16[:, 0:P], parts[:, :], ident16[:, :]).then_inc(partsT_filled, 1)
                    if not (isinstance(s, int) and s == 0 and j == 0):
                        turn((j + 1) % 2, g - 1)
                    if nxt:
                        project(np_, nj, job(s, j, 0), (1,))
                    pe.wait_ge(partsT_ready, g + 1)
                    if j > 0:
                        pe.wait_ge(state_ready, s * 6 + 2 * j)
                    for half in range(2):
                        spread(BK[half][:, :], half * HB, j).then_inc(qrms_filled, 1)
                    if j > 0:
                        attend(s, par, j - 1)
                    elif not (isinstance(s, int) and s == 0):
                        attend(s - 1, 1 - par, NT - 1)
                    for half in range(2):
                        spread(SC[:, half * BANK:(half + 1) * BANK], H + half * HB, j).then_inc(krms_filled, 1)
                    if j == 1:
                        v_stage(s)
                    if nxt:
                        project(np_, nj, job(s, j, 0), (2,))
                    if j == 2 and not last_s:
                        z_stage(s + 1, 1 - par)
                    for half in range(2):
                        pe.wait_ge(pq_ready, g * 2 + half + 1)
                        pe.wait_ge(krms_ready, g * 2 + half + 1)
                        for h in range(half * HB, (half + 1) * HB):
                            last = pe.matmul(SC[:, h * P:(h + 1) * P], p_q[j % 2][:, h, :],
                                             xT[par][:, 1 + j * P:1 + (j + 1) * P], start=True, stop=True)
                        last.then_inc(scores_filled, 1)
                    if j == 0 and not (isinstance(s, int) and s == 0):
                        finish(s - 1)
                    if j > 0:
                        for h in range(H):
                            if h % HB == 0:
                                pe.wait_ge(pdec_ready, s * 6 + 2 * (j - 1) + h // HB + 1)
                            last = pe.matmul(OUT[:, j * P:(j + 1) * P], state[:, h, :], p_dec[:, h, :],
                                             start=(h == 0), stop=False)
                        last.then_inc(cross_done, 1)
                    if nxt:
                        project(np_, nj, job(s, j, 0), (3,))
                    if j < NT - 1:
                        for half in range(2):
                            pe.wait_ge(vscaled_ready, s * 6 + 2 * j + half + 1)
                            pe.matmul(BK[half][:, :], xn[par][:, j, :],
                                      v_scaled[:, half * BANK:(half + 1) * BANK], start=True, stop=True)\
                                .then_inc(incr_filled, 1)
                    if nxt:
                        project(np_, nj, job(s, j, 0), (4, 5))
                    if j == 1 and not last_s:
                        pe.wait_ge(ffn_ready, s + 1)
                        xT_stage(s + 1, 1 - par)
                    if j == 2 and not last_s:
                        gate_stage(s + 1)
                        p_stage(s + 1, 1 - par, (0, 1), job(s, j, 6))
                        r_stage(s + 1)
                        p_stage(s + 1, 1 - par, (2,), job(s, j, 8))
                        k_stage(s + 1)
                        p_stage(s + 1, 1 - par, (3,), job(s, j, 9))
                    if j == 3 and not last_s:
                        p_stage(s + 1, 1 - par, range(HB, H), job(s, j, 6))
            sequences(pe, run)
            turn(1, NSEQ * NT - 1)
            attend(NSEQ - 1, 1, NT - 1)
            finish(NSEQ - 1)

        @block.scalar
        def _(act):
            for n in SPLIT_JOBS:
                act.wait_ge(setup_filled, n + 1)
                act.activation(split_dst(n, True), PJ[n % 2][:, :], ACT.Copy).then_inc(setup_hi, 1)

            def norm_stage(s):
                act.wait_ge(var_ready, s + 1)
                act.activation(ln_var[:, :], mean_var[:, :, 1], ACT.Ln, bias=eps[:, 0:1]).then_inc(lnvar_done, 1)
                act.wait_ge(lnvar_done, s + 1)
                act.activation(rstd[:, :], ln_var[:, :], ACT.Exp, scale=-0.5).then_inc(rstd_ready, 1)

            def xT_stage(s, par):
                act.wait_ge(xT_filled, s + 1)
                act.activation(xT[par][:, 1:1 + T], MI[:, :], ACT.Copy).then_inc(xT_ready, 1)
                act.activation(xT_hi[par][:, :], MI[:, :], ACT.Copy).then_inc(xhi_ready, 1)

            def mix_stage(s, par):
                act.wait_ge(xT_ready, s + 1)
                act.wait_ge(small_ready, 2)
                need(act, xrk_ready, s)
                act.activation(mix_r[:, :], xT[par][:, 0:T], ACT.Copy, scale=one_minus_mu[:, 0:1]).then_inc(mix_ready, 1)
                act.activation(mix_k[:, :], xT[par][:, 0:T], ACT.Copy, scale=one_minus_mu[:, 1:2]).then_inc(mix_ready, 1)

            def gate_log_stage(s):
                act.wait_ge(zneg_ready, s + 1)
                act.activation(z_l1p[:, :, :], z_neg[:, :, :], ACT.Exp).then_inc(zexp_done, 1)
                act.wait_ge(zexp_done, s + 1)
                act.activation(z_l1p[:, :, :], z_l1p[:, :, :], ACT.Ln, bias=1.0).then_inc(zl1p_ready, 1)

            def decay_stage(s, par):
                act.wait_ge(gates_filled, s + 1)
                n = NT * H
                act.activation(q_decay[par][:, :, :, 1], MI[:, 0:n].rearrange("p (j h) -> p j h", j=NT), ACT.Exp)
                act.activation(decay[par][:, :, :, :].rearrange("p k j h -> p (k j h)"), MI[:, n:3 * n], ACT.Exp)\
                    .then_inc(decay_ready, 1)

            def r_stage(s):
                act.wait_ge(r_filled, s + 1)
                need(act, rone_done, s)
                act.activation(r_exp[:, :], MI[:, :], ACT.Exp, scale=-1.0).then_inc(rexp_ready, 1)

            def k_stage(s):
                act.wait_ge(k_filled, s + 1)
                act.activation(k_relu[:, :], MI[:, :], ACT.Relu).then_inc(krelu_ready, 1)
                act.wait_ge(krelu_ready, s + 1)
                need(act, v_filled, s)
                act.activation(k_act[:, :], k_relu[:, :], ACT.Square).then_inc(kact_ready, 1)

            def f_stage(s):
                act.wait_ge(ffn_ready, s + 1)
                act.activation(f_exp[:, :], ffn[:, :], ACT.Exp, scale=-1.0).then_inc(fexp_ready, 1)

            def p_stage(s, par, hs, first_job):
                for i, h in enumerate(hs):
                    act.wait_ge(proj_filled, first_job + i + 1)
                    act.activation(p_raw[par][:, h, :], PJ[h % 2][:, :], ACT.Copy).then_inc(proj_read, 1)

            def squares(b, first_job, k):
                act.wait_ge(proj_filled, first_job + k + 1)
                for i in range(HB):
                    last = act.activation(squared[:, k * HB + i, :], PJ[k % 2][:, i * D:(i + 1) * D], ACT.Square,
                                          accum_out=ssq[b][:, k * HB + i:k * HB + i + 1])
                last.then_inc(proj_read, 1)

            def rms_stage(b, first_job, count):
                act.wait_ge(proj_read, first_job + 4)
                act.activation(ln_ms[:, :], ssq[b][:, :], ACT.Ln, bias=eps[:, 1:2], scale=1.0 / DK)\
                    .then_inc(lnms_done, 1)
                act.wait_ge(lnms_done, count)
                act.activation(rms[b][:, :], ln_ms[:, :], ACT.Exp, scale=-0.5).then_inc(rms_ready, 1)

            def v_stage(b, first_job, tiles_done):
                need(act, av_done, tiles_done)
                for k in (4, 5):
                    act.wait_ge(proj_filled, first_job + k + 1)
                    act.activation(vp[b][:, (k - 4) * BANK:(k - 3) * BANK], PJ[k % 2][:, :], ACT.Copy)\
                        .then_inc(proj_read, 1)

            act.preload_act_table_set("natural_log_exp_and_others")
            act.wait_ge(small_ready, 2)
            norm_stage(0)
            xT_stage(0, 0)
            mix_stage(0, 0)
            gate_log_stage(0)
            decay_stage(0, 0)
            r_stage(0)
            k_stage(0)
            p_stage(0, 0, range(H), 0)
            for k in range(4):
                squares(0, 2 * HB, k)
            rms_stage(0, 2 * HB, 1)
            v_stage(0, 2 * HB, 0)

            def attT_stage(b, g):
                for half in range(2):
                    act.wait_ge(attT_filled, g * 2 + half + 1)
                    act.activation(attT[b][:, half * HB:(half + 1) * HB, :],
                                   SCh[:, half * HB:(half + 1) * HB, :], ACT.Copy).then_inc(attT_ready, 1)

            def run(s, par, last_s):
                for j in range(NT):
                    g = s * NT + j
                    nxt = not (last_s and j == NT - 1)
                    nb = (j + 1) % 2
                    if nxt:
                        squares(nb, job(s, j, 0), 0)
                    if not (isinstance(s, int) and s == 0 and j == 0):
                        attT_stage(nb, g - 1)
                    if nxt:
                        squares(nb, job(s, j, 0), 1)
                    for half in range(2):
                        act.wait_ge(krms_filled, g * 2 + half + 1)
                        act.activation(k_rms[j % 2][:, half * BANK:(half + 1) * BANK],
                                       SC[:, half * BANK:(half + 1) * BANK], ACT.Copy).then_inc(krms_ready, 1)
                    if nxt:
                        squares(nb, job(s, j, 0), 2)
                    if j == 0 and not last_s:
                        norm_stage(s + 1)
                    if j == 2 and not last_s:
                        mix_stage(s + 1, 1 - par)
                    if nxt:
                        squares(nb, job(s, j, 0), 3)
                    if j == 2 and not last_s:
                        gate_log_stage(s + 1)
                    act.wait_ge(shifted_ready, g + 1)
                    act.activation(own[j % 2][:, :, :], own[j % 2][:, :, :], ACT.Exp, scale=SCALE)\
                        .then_inc(exp_ready, 1)
                    if nxt:
                        rms_stage(nb, job(s, j, 0), g + 2)
                        v_stage(nb, job(s, j, 0), g)
                    if j == 1 and not last_s:
                        xT_stage(s + 1, 1 - par)
                    if j == 1:
                        f_stage(s)
                    if j == 2 and not last_s:
                        decay_stage(s + 1, 1 - par)
                        p_stage(s + 1, 1 - par, (0, 1), job(s, j, 6))
                        r_stage(s + 1)
                        p_stage(s + 1, 1 - par, (2,), job(s, j, 8))
                        k_stage(s + 1)
                        p_stage(s + 1, 1 - par, (3,), job(s, j, 9))
                    if j == 3 and not last_s:
                        p_stage(s + 1, 1 - par, range(HB, H), job(s, j, 6))

            sequences(act, run)
            attT_stage(1, NSEQ * NT - 1)

        @block.vector
        def _(dve):
            dve.memset(eps[:, 0:1], LN_EPS)
            dve.memset(eps[:, 1:2], RMS_EPS).then_inc(small_ready, 1)
            dve.memset(parts[:, :], 0.0)
            for b in range(2):
                dve.memset(xT[b][:, 0:1], 0.0)
                dve.memset(att[b][:, :, :], 0.0)
                dve.memset(q_decay[b][:, :, :, 0], 1.0)
            dve.memset(span[:, :, :], 0.0).then_inc(zeroed, 1)
            dve.wait_ge(zeroed, 1)
            dve.memset(span[0:CH, 0, :], 1.0)
            dve.memset(span[:, 1, :], 1.0)
            dve.memset(span[CH:P, 2, 0:CH], 1.0).then_inc(consts_ready, 1)
            dve.wait_ge(weights_in, NWEIGHTS)
            dve.tensor_scalar(one_minus_mu[:, :], mu[:, :], -1.0, 1.0, ALU.mult, ALU.add).then_inc(small_ready, 1)

            def norm_stats(s, par, loads):
                dve.wait_ge(x_in[par], loads)
                for j in range(NT):
                    last = dve.bn_stats(stats[:, j, :], xs[par][:, j, :])
                last.then_inc(stats_done, 1)
                dve.wait_ge(stats_done, s + 1)
                dve.memset(scratch[:, :], 0.0)
                for j in range(NT):
                    last = dve.bn_aggr(mean_var[:, j, :], stats[:, j, :])
                last.then_inc(var_ready, 1)

            def norm_stage(s, par):
                dve.wait_ge(var_ready, s + 1)
                dve.wait_ge(rstd_ready, s + 1)
                for j in range(NT):
                    last = dve.tensor_scalar(xn[par][:, j, :], xs[par][:, j, :], mean_var[:, j, 0:1],
                                             rstd[:, j:j + 1], ALU.subtract, ALU.mult)
                last.then_inc(xn_ready, 1)

            def xlo_stage(s, par):
                dve.wait_ge(xhi_ready, s + 1)
                dve.tensor_tensor(xT_lo[par][:, :], xT[par][:, 1:1 + T], xT_hi[par][:, :].bitcast(F32),
                                  ALU.subtract).then_inc(xlo_ready, 1)

            def mix_stage(s, par):
                dve.wait_ge(mix_ready, s * 2 + 2)
                need(dve, k_filled, s)
                dve.scalar_tensor_tensor(xr[:, :], xT[par][:, 1:1 + T], mu[:, 0:1], mix_r[:, :], ALU.mult, ALU.add)
                dve.scalar_tensor_tensor(xk[:, :], xT[par][:, 1:1 + T], mu[:, 1:2], mix_k[:, :], ALU.mult, ALU.add)\
                    .then_inc(xrk_ready, 1)

            def z_stage(s):
                dve.wait_ge(z_filled, s + 1)
                dve.tensor_tensor(zb[:, :, :], MI[:, 0:NT * H].rearrange("p (j h) -> p j h", j=NT),
                                  bg_all[:, :].rearrange("p (o h) -> p o h", o=1).broadcast_to([P, NT, H]), ALU.add)\
                    .then_inc(zb_done, 1)
                dve.wait_ge(zb_done, s + 1)
                dve.scalar_tensor_tensor(z_neg[:, :, :], zb[:, :, :], -1.0, zb[:, :, :], ALU.mult, ALU.min)\
                    .then_inc(zneg_ready, 1)

            def gate_stage(s):
                dve.wait_ge(zl1p_ready, s + 1)
                dve.scalar_tensor_tensor(log_g[:, :, :], zb[:, :, :], 0.0, z_l1p[:, :, :], ALU.min, ALU.subtract)\
                    .then_inc(logg_ready, 1)

            HALF = T // 2

            def r_stage(s, half):
                if half == 0:
                    dve.wait_ge(rexp_ready, s + 1)
                    need(dve, ffn_ready, s)
                    dve.tensor_scalar(r_sig[:, :], r_exp[:, :], 1.0, None, ALU.add).then_inc(rone_done, 1)
                    dve.wait_ge(rone_done, s + 1)
                t = slice(half * HALF, (half + 1) * HALF)
                dve.reciprocal(r_sig[:, t], r_sig[:, t]).then_inc(rsig_done, 1)

            def v_stage(s):
                dve.wait_ge(v_filled, s + 1)
                dve.wait_ge(rsig_done, s * 2 + 2)
                dve.tensor_tensor(ffn[:, :], MI[:, :], r_sig[:, :], ALU.mult).then_inc(ffn_ready, 1)

            def f_stage(s, half):
                if half == 0:
                    dve.wait_ge(fexp_ready, s + 1)
                    dve.tensor_scalar(f_exp[:, :], f_exp[:, :], 1.0, None, ALU.add).then_inc(fone_done, 1)
                    dve.wait_ge(fone_done, s + 1)
                t = slice(half * HALF, (half + 1) * HALF)
                dve.reciprocal(f_exp[:, t], f_exp[:, t]).then_inc(fsig_done, 1)

            def silu_stage(s, par):
                dve.wait_ge(fsig_done, s * 2 + 2)
                dve.tensor_tensor(gT[par][:, :], ffn[:, :], f_exp[:, :], ALU.mult).then_inc(gT_ready, 1)

            def split_factors(b, count):
                dve.wait_ge(rms_ready, count)
                need(dve, partsT_filled, count - 1)
                dve.tensor_scalar(rms[b][:, 0:H], rms[b][:, 0:H], gain_all[:, 0:1], None, ALU.mult).then_inc(gained, 1)
                dve.wait_ge(gained, count)
                dve.tensor_copy(parts[:, 0:NR], rms[b][:, :]).then_inc(split_step, 1)
                dve.wait_ge(split_step, count * 4 - 3)
                dve.tensor_tensor(res1[:, :], rms[b][:, :], parts[:, 0:NR], ALU.subtract).then_inc(split_step, 1)
                dve.wait_ge(split_step, count * 4 - 2)
                dve.tensor_copy(parts[:, NR:2 * NR], res1[:, :]).then_inc(split_step, 1)
                dve.wait_ge(split_step, count * 4 - 1)
                dve.tensor_tensor(res2[:, :], res1[:, :], parts[:, NR:2 * NR], ALU.subtract).then_inc(split_step, 1)
                dve.wait_ge(split_step, count * 4)
                dve.tensor_copy(parts[:, 2 * NR:3 * NR], res2[:, :]).then_inc(parts_ready, 1)

            y_flat = y[:, :, :].rearrange("p j d -> p (j d)")
            norm_stats(0, 0, 16)
            for n in range(11):
                dve.wait_ge(setup_filled, n + 1)
                if n in SPLIT_JOBS:
                    dve.wait_ge(setup_hi, SPLIT_JOBS.index(n) + 1)
                    last = dve.tensor_tensor(split_dst(n, False), PJ[n % 2][:, :], split_dst(n, True).bitcast(F32),
                                             ALU.subtract)
                elif n < 6:
                    last = dve.tensor_copy(woT[:, (n - 4) * HB:(n - 3) * HB, :].rearrange("p h d -> p (h d)"),
                                           PJ[n % 2][:, :])
                else:
                    last = dve.tensor_copy(small_wT[:, :], PJ[n % 2][:, 0:3 * D + H])
                last.then_inc(setup_read, 1)
            norm_stage(0, 0)
            xlo_stage(0, 0)
            z_stage(0)
            gate_stage(0)
            mix_stage(0, 0)
            split_factors(0, 1)
            r_stage(0, 0)

            def run(s, par, last_s):
                first = isinstance(s, int) and s == 0
                for j in range(NT):
                    g = s * NT + j
                    b = j % 2
                    dve.wait_ge(partsT_filled, g + 1)
                    dve.tensor_copy(partsT[b][:, :], MI16[:, 0:P]).then_inc(partsT_ready, 1)
                    if j == 0 and not first:
                        dve.wait_ge(av_done, g)
                        dve.wait_ge(gT_ready, s)
                        dve.tensor_tensor(sgT[:, :], OUT[:, :], gT[1 - par][:, :], ALU.mult).then_inc(sg_ready, 1)
                    if j == 0:
                        dve.wait_ge(proj_read, p_job(s, H - 1) + 1)
                    for half in range(2):
                        dve.wait_ge(qrms_filled, g * 2 + half + 1)
                        hs = slice(half * HB, (half + 1) * HB)
                        dve.tensor_tensor(p_q[b][:, hs, :], p_raw[par][:, hs, j * P:(j + 1) * P],
                                          BK[half][:, :].rearrange("p (h t) -> p h t", h=HB), ALU.mult)\
                            .then_inc(pq_ready, 1)
                    if j == 0:
                        if not last_s:
                            norm_stats(s + 1, 1 - par, x_loads(s, par))
                        r_stage(s, 1)
                    if j == 1:
                        if not last_s:
                            norm_stage(s + 1, 1 - par)
                        v_stage(s)
                    if j == 2:
                        if not last_s:
                            xlo_stage(s + 1, 1 - par)
                            z_stage(s + 1)
                        f_stage(s, 0)
                    if j == 3:
                        f_stage(s, 1)
                        if not last_s:
                            r_stage(s + 1, 0)
                    dve.wait_ge(krms_ready, g * 2 + 2)
                    dve.wait_ge(scores_filled, g * 2 + 2)
                    kr = k_rms[b][:, :].rearrange("p (h s) -> p h s", h=H)
                    dve.tensor_tensor(own[b][0:CH, :, :], SCh[0:CH, :, 0:CH], kr[0:CH, :, 0:CH], ALU.mult)
                    dve.tensor_tensor(own[b][CH:P, :, :], SCh[CH:P, :, CH:P], kr[CH:P, :, CH:P], ALU.mult)\
                        .then_inc(own_ready, 1)
                    dve.wait_ge(own_ready, g + 1)
                    dve.tensor_tensor(own[b][:, :, :], own[b][:, :, :],
                                      mask[:, :].rearrange("p (o s) -> p o s", o=1).broadcast_to([P, H, CH]),
                                      ALU.add).then_inc(mask_ready, 1)
                    dve.wait_ge(mask_ready, g + 1)
                    dve.tensor_reduce(top[:, :], own[b][:, :, :], AX.X, ALU.max).then_inc(top_done, 1)
                    dve.wait_ge(top_done, g + 1)
                    dve.tensor_tensor(own[b][:, :, :], own[b][:, :, :], over(top), ALU.subtract)\
                        .then_inc(shifted_ready, 1)
                    dve.tensor_tensor(att[b][CH:P, :, 0:CH], SCh[CH:P, :, 0:CH], kr[CH:P, :, 0:CH], ALU.mult)
                    if j == 2 and not last_s:
                        gate_stage(s + 1)
                    dve.wait_ge(exp_ready, g + 1)
                    dve.tensor_reduce(total[:, :], own[b][:, :, :], AX.X, ALU.add).then_inc(total_done, 1)
                    dve.wait_ge(total_done, g + 1)
                    dve.reciprocal(inv_total[b][:, :], total[:, :]).then_inc(inv_ready, 1)
                    dve.wait_ge(inv_ready, g + 1)
                    dve.tensor_tensor(att[b][0:CH, :, 0:CH], own[b][0:CH, :, :], over(inv_total[b])[0:CH, :, :],
                                      ALU.mult).then_inc(att_a_ready, 1)
                    if not (last_s and j == NT - 1):
                        split_factors((j + 1) % 2, g + 2)
                    if j == 2 and not last_s:
                        mix_stage(s + 1, 1 - par)
                    if j == 3:
                        silu_stage(s, par)
                    if j == 0 and not first:
                        dve.wait_ge(outT_filled, s)
                        dve.wait_ge(residual_in, s * 16)
                        dve.tensor_tensor(y_flat, OUT[:, :], y_flat, ALU.add)\
                            .then_inc(y_ready, 1)
                    if j < NT - 1:
                        dve.wait_ge(decay_ready, s + 1)
                        for half in range(2):
                            dve.wait_ge(incr_filled, s * 6 + 2 * j + half + 1)
                            if j == 0:
                                last = dve.tensor_copy(
                                    state[:, half * HB:(half + 1) * HB, :].rearrange("p h d -> p (h d)"),
                                    BK[half][:, :])
                            else:
                                if half == 0:
                                    dve.wait_ge(state_ready, s * 6 + 2 * j)
                                for i in range(HB):
                                    h = half * HB + i
                                    last = dve.scalar_tensor_tensor(
                                        state[:, h, :], state[:, h, :], decay[par][:, 0, j, h:h + 1],
                                        BK[half][:, i * D:(i + 1) * D], ALU.mult, ALU.add)
                            last.then_inc(state_ready, 1)

            def x_loads(s, par):
                return s * 8 + (16 if par == 0 else 24)

            def over(v):
                return v[:, :].rearrange("p (h o) -> p h o", o=1).broadcast_to([P, H, CH])

            sequences(dve, run)
            dve.wait_ge(av_done, NSEQ * NT)
            dve.wait_ge(gT_ready, NSEQ)
            dve.tensor_tensor(sgT[:, :], OUT[:, :], gT[1][:, :], ALU.mult).then_inc(sg_ready, 1)
            dve.wait_ge(outT_filled, NSEQ)
            dve.wait_ge(residual_in, 16 * NSEQ)
            dve.tensor_tensor(y_flat, OUT[:, :], y_flat, ALU.add).then_inc(y_ready, 1)

        @block.gpsimd
        def _(pool):
            pool.memset(ident[:, :], 0.0)
            pool.memset(ident16[:, :], 0.0)
            pool.memset(mask[:, :], 0.0)
            pool.memset(pick[:, :, :], 0.0).then_inc(pick_ready, 1)
            pool.wait_ge(pick_ready, 1)
            for m in (ident, ident16):
                pool.affine_select(out=m[:, :], in_=m[:, :], compare_op=ALU.not_equal, fill=1.0, base=0,
                                   pattern=[[-1, P]], channel_multiplier=1).then_inc(pick_ready, 1)
            for a in range(2):
                pool.wait_ge(pick_ready, 3 + a)
                rows = mask[a * CH:(a + 1) * CH, :]
                pool.affine_select(out=rows, in_=rows, compare_op=ALU.is_ge, fill=MASKED, base=0,
                                   pattern=[[-1, CH]], channel_multiplier=1).then_inc(pick_ready, 1)
            for part in range(3):
                pool.wait_ge(pick_ready, part + 5)
                pool.affine_select(out=pick[:, :, :], in_=pick[:, :, :], compare_op=ALU.not_equal, fill=1.0,
                                   base=-part * NR, pattern=[[-1, NR], [0, P]], channel_multiplier=1)\
                    .then_inc(pick_ready, 1)

            def run(s, par, last_s):
                for j in range(NT):
                    g = s * NT + j
                    b = j % 2
                    if j == 0:
                        pool.wait_ge(decay_ready, s + 1)
                    need(pool, att_b_ready, g)
                    if j < NT - 1:
                        pool.wait_ge(rms_ready, g + 1)
                        need(pool, incr_filled, s * 6 + 2 * j)
                        pool.tensor_tensor(v_scale[:, :], rms[b][:, H:NR], decay[par][:, 1, j, :], ALU.mult)\
                            .then_inc(vscale_done, 1)
                        pool.wait_ge(vscale_done, s * 3 + j + 1)
                        pool.wait_ge(proj_read, tile_job(s, j, 5) + 1)
                        for half in range(2):
                            hs = slice(half * HB, (half + 1) * HB)
                            cs = slice(half * BANK, (half + 1) * BANK)
                            pool.tensor_tensor(
                                v_scaled[:, cs].rearrange("p (h d) -> p h d", h=HB),
                                vp[b][:, cs].rearrange("p (h d) -> p h d", h=HB),
                                v_scale[:, hs].rearrange("p (h o) -> p h o", o=1).broadcast_to([P, HB, D]),
                                ALU.mult).then_inc(vscaled_ready, 1)
                    if j > 0:
                        need(pool, cross_done, s * 3 + j - 1)
                        for half in range(2):
                            pool.wait_ge(pq_ready, g * 2 + half + 1)
                            hs = slice(half * HB, (half + 1) * HB)
                            pool.tensor_tensor(
                                p_dec[:, hs, :].rearrange("p h (a t) -> p (h a) t", a=2),
                                p_q[b][:, hs, :].rearrange("p h (a t) -> p (h a) t", a=2),
                                q_decay[par][:, j, hs, :].rearrange("p h (a o) -> p (h a) o", o=1)
                                .broadcast_to([P, 2 * HB, CH]), ALU.mult).then_inc(pdec_ready, 1)
                    if j > 0:
                        pool.wait_ge(pdec_ready, s * 6 + 2 * j)
                    else:
                        pool.wait_ge(vscaled_ready, s * 6 + 2)
                    pool.wait_ge(inv_ready, g + 1)
                    pool.tensor_tensor(att[b][CH:P, :, CH:P], own[b][CH:P, :, :],
                                       inv_total[b][CH:P, :].rearrange("p (h o) -> p h o", o=1)
                                       .broadcast_to([CH, H, CH]), ALU.mult).then_inc(att_b_ready, 1)

            sequences(pool, run)


_INS = ["x", "Wq", "Wk", "Wv", "Wg", "bg", "Wo", "gain", "Wr", "Wkf", "Wvf", "mu_r", "mu_k"]


def kernel(L0_attn_x, L0_attn_Wq, L0_attn_Wk, L0_attn_Wv, L0_attn_Wg, L0_attn_bg, L0_attn_Wo, L0_attn_qk_gain,
           L0_ffn_W_r, L0_ffn_W_k, L0_ffn_W_v, L0_ffn_mu_r, L0_ffn_mu_k):
    import concourse.bacc as bacc
    from concourse.bass_utils import run_bass_kernel_spmd

    values = [L0_attn_x, L0_attn_Wq, L0_attn_Wk, L0_attn_Wv, L0_attn_Wg, L0_attn_bg, L0_attn_Wo,
              np.asarray(L0_attn_qk_gain).reshape(1), L0_ffn_W_r, L0_ffn_W_k, L0_ffn_W_v, L0_ffn_mu_r, L0_ffn_mu_k]
    nc = bacc.Bacc("TRN2", target_bir_lowering=False, num_devices=1)
    arrays, args = {}, []
    for name, value in zip(_INS, values):
        a = np.ascontiguousarray(value)
        arrays[f"in_{name}"] = a
        args.append(nc.dram_tensor(f"in_{name}", a.shape, mybir.dt.from_np(a.dtype), kind="ExternalInput").ap())
    shape = arrays["in_x"].shape
    args.append(nc.dram_tensor("out", shape, F32, kind="ExternalOutput").ap())
    build(nc, *args)
    r = run_bass_kernel_spmd(nc, [arrays], core_ids=[0])
    return r.results[0]["out"]
```

```python
from contextlib import ExitStack

import numpy as np
import concourse.bass as bass
from concourse import mybir

F32 = mybir.dt.float32
F32R = mybir.dt.float32r
BF16 = mybir.dt.bfloat16
ALU = mybir.AluOpType
ACT = mybir.ActivationFunctionType
AX = mybir.AxisListType

P = 128
CH = 64
BANK = 512
MASKED = -1.0e30
LN_EPS = 1.0e-5
RMS_EPS = 1.0e-6


def build(nc, x, Wq, Wk, Wv, Wg, bg, Wo, gain, Wr, Wkf, Wvf, mu_r, mu_k, out):
    NSEQ, T, D = x.shape
    H = Wg.shape[0]
    DK = Wq.shape[0] // H
    NT = T // P
    HW = H * D
    HB = BANK // D
    assert D == P and DK == P and T == BANK and H == 2 * HB and NT == 4 and NSEQ % 2 == 0
    SCALE = 1.0 / float(np.sqrt(DK))
    NR = 2 * H

    with ExitStack() as ctx:
        def sb(name, shape, dt=F32):
            return ctx.enter_context(nc.sbuf_tensor(name, shape, dt))

        def pair(name, shape, dt=F32):
            return [sb(f"{name}{i}", shape, dt) for i in range(2)]

        def bank(name, n=1):
            return ctx.enter_context(nc.psum_tensor(name, [P, n * BANK], F32))

        def sem(name):
            return ctx.enter_context(nc.semaphore(name))

        wqk_in = sb("wqk_in", [P, 2 * H, D])
        wq_in, wk_in = wqk_in[:, 0:H, :], wqk_in[:, H:2 * H, :]
        wv_in = sb("wv_in", [P, H, D])
        wo_in = sb("wo_in", [P, HW])
        wg_in = sb("wg_in", [H, D])
        ffn_in = sb("ffn_in", [P, 3, D])
        bg_all = sb("bg_all", [P, H])
        gain_all = sb("gain_all", [P, 1])
        mu = sb("mu", [P, 2])
        one_minus_mu = sb("one_minus_mu", [P, 2])
        eps = sb("eps", [P, 2])
        scratch = sb("scratch", [P, 1])
        mask = sb("mask", [P, HB, P], BF16)
        ident = sb("ident", [P, P])
        ident16 = sb("ident16", [P, P], BF16)
        pick = sb("pick", [P, NR, P], BF16)
        span = sb("span", [P, 3, P])
        woT = sb("woT", [P, H, D])
        small_wT = sb("small_wT", [P, 3 * D + H])
        w_hi = sb("w_hi", [P, 3 * HW], F32R)
        w_lo = sb("w_lo", [P, 3 * HW], F32R)
        a_hi = sb("a_hi", [P, HW], F32R)
        a_lo = sb("a_lo", [P, HW], F32R)
        xs = pair("xs", [P, NT, D])
        stats = sb("stats", [P, NT, 6])
        mean_var = sb("mean_var", [P, NT, 2])
        ln_var = sb("ln_var", [P, NT])
        rstd = sb("rstd", [P, NT])
        xn = pair("xn", [P, NT, D])
        xT = pair("xT", [P, 1 + T])
        xT_hi = pair("xT_hi", [P, T], F32R)
        xT_lo = pair("xT_lo", [P, T], F32R)
        p_raw = pair("p_raw", [P, H, T])
        mix_r = sb("mix_r", [P, T])
        mix_k = sb("mix_k", [P, T])
        xr = sb("xr", [P, T])
        xk = sb("xk", [P, T])
        r_exp = sb("r_exp", [P, T])
        r_sig = sb("r_sig", [P, T])
        k_relu = sb("k_relu", [P, T])
        k_act = sb("k_act", [P, T])
        ffn = sb("ffn", [P, T])
        f_exp = sb("f_exp", [P, T])
        gT = pair("gT", [P, T])
        zb = sb("zb", [P, NT, H])
        z_neg = sb("z_neg", [P, NT, H])
        z_l1p = sb("z_l1p", [P, NT, H])
        log_g = sb("log_g", [P, NT, H])
        decay = pair("decay", [P, 2, NT, H])
        q_decay = pair("q_decay", [P, NT, H, 2])
        sgT = sb("sgT", [P, T])
        y = sb("y", [P, NT, D])
        squared = wqk_in
        ssq = pair("ssq", [P, NR])
        ln_ms = sb("ln_ms", [P, NR])
        rms = pair("rms", [P, NR])
        res1 = sb("res1", [P, NR])
        res2 = sb("res2", [P, NR])
        parts = sb("parts", [P, P], BF16)
        partsT = pair("partsT", [P, P], BF16)
        vp = pair("vp", [P, HW])
        v_scale = sb("v_scale", [P, H])
        v_scaled = sb("v_scaled", [P, HW])
        k_rms = pair("k_rms", [P, HW])
        p_q = pair("p_q", [P, H, P])
        p_dec = sb("p_dec", [P, H, P])
        own = pair("own", [P, H, CH])
        top = sb("top", [P, H])
        total = sb("total", [P, H])
        inv_total = pair("inv_total", [P, H])
        att = pair("att", [P, H, P])
        attT = pair("attT", [P, H, P])
        state = sb("state", [P, H, D])

        PJ = [bank("PJ0"), bank("PJ1")]
        SC = bank("SC", 2)
        BK = [bank("BK0"), bank("BK1")]
        OUT = bank("OUT")
        MI = bank("MI")
        SCh = SC[:, :].rearrange("p (h s) -> p h s", h=H)
        MI16 = MI[:, :].bitcast(BF16)

        weights_in = sem("weights_in")
        x_in = [sem("x_in0"), sem("x_in1")]
        residual_in = sem("residual_in")
        y_out = sem("y_out")
        zeroed = sem("zeroed")
        consts_ready = sem("consts_ready")
        pick_ready = sem("pick_ready")
        small_ready = sem("small_ready")
        setup_filled = sem("setup_filled")
        setup_hi = sem("setup_hi")
        setup_read = sem("setup_read")
        stats_done = sem("stats_done")
        var_ready = sem("var_ready")
        lnvar_done = sem("lnvar_done")
        rstd_ready = sem("rstd_ready")
        xn_ready = sem("xn_ready")
        xT_filled = sem("xT_filled")
        xT_ready = sem("xT_ready")
        xhi_ready = sem("xhi_ready")
        xlo_ready = sem("xlo_ready")
        z_filled = sem("z_filled")
        zb_done = sem("zb_done")
        zneg_ready = sem("zneg_ready")
        zexp_done = sem("zexp_done")
        zl1p_ready = sem("zl1p_ready")
        logg_ready = sem("logg_ready")
        gates_filled = sem("gates_filled")
        decay_ready = sem("decay_ready")
        mix_ready = sem("mix_ready")
        xrk_ready = sem("xrk_ready")
        r_filled = sem("r_filled")
        rexp_ready = sem("rexp_ready")
        k_filled = sem("k_filled")
        krelu_ready = sem("krelu_ready")
        kact_ready = sem("kact_ready")
        rone_done = sem("rone_done")
        rsig_done = sem("rsig_done")
        v_filled = sem("v_filled")
        ffn_ready = sem("ffn_ready")
        fexp_ready = sem("fexp_ready")
        fone_done = sem("fone_done")
        fsig_done = sem("fsig_done")
        gT_ready = sem("gT_ready")
        proj_filled = sem("proj_filled")
        proj_read = sem("proj_read")
        lnms_done = sem("lnms_done")
        rms_ready = sem("rms_ready")
        gained = sem("gained")
        split_step = sem("split_step")
        parts_ready = sem("parts_ready")
        partsT_filled = sem("partsT_filled")
        partsT_ready = sem("partsT_ready")
        krms_filled = sem("krms_filled")
        krms_ready = sem("krms_ready")
        qrms_filled = sem("qrms_filled")
        pq_ready = sem("pq_ready")
        vscale_done = sem("vscale_done")
        vscaled_ready = sem("vscaled_ready")
        pdec_ready = sem("pdec_ready")
        scores_filled = sem("scores_filled")
        own_ready = sem("own_ready")
        top_done = sem("top_done")
        shifted_ready = sem("shifted_ready")
        exp_ready = sem("exp_ready")
        total_done = sem("total_done")
        inv_ready = sem("inv_ready")
        att_a_ready = sem("att_a_ready")
        att_b_ready = sem("att_b_ready")
        attT_filled = sem("attT_filled")
        attT_ready = sem("attT_ready")
        cross_done = sem("cross_done")
        av_done = sem("av_done")
        incr_filled = sem("incr_filled")
        state_ready = sem("state_ready")
        sg_ready = sem("sg_ready")
        outT_filled = sem("outT_filled")
        y_ready = sem("y_ready")

        block = ctx.enter_context(nc.Block())

        def need(eng, s, n):
            if not (isinstance(n, int) and n <= 0):
                eng.wait_ge(s, n)

        def job(s, j, k):
            return H + 6 + s * 32 + (0, 6, 12, 22)[j] + k

        def v_at(s, j):
            return 4 if j < 2 or (isinstance(s, int) and s == NSEQ - 1) else 6

        def p_at(i):
            return (4, 5, 8, 9)[i]

        def v_jobs(s, j):
            if j > 0:
                return job(s, j - 1, v_at(s, j - 1)) + 2
            if isinstance(s, int) and s == 0:
                return H + 6
            return job(s - 1, NT - 1, v_at(s - 1, NT - 1)) + 2

        def p_heads(j, i):
            return ((j - 2) * HB + i,)

        def sequences(eng, run):
            run(0, 0, False)
            run(1, 1, False)
            with eng.Fori(1, NSEQ // 2 - 1) as i:
                run(i * 2, 0, False)
                run(i * 2 + 1, 1, False)
            run(NSEQ - 2, 0, False)
            run(NSEQ - 1, 1, True)

        SPLIT_JOBS = (0, 1, 2, 3, 7, 8, 9, 10)

        def split_dst(n, hi):
            cols = {0: 0, 1: BANK, 2: HW, 3: HW + BANK, 9: 2 * HW, 10: 2 * HW + BANK}
            if n in cols:
                t, c = (w_hi if hi else w_lo), cols[n]
            else:
                t, c = (a_hi if hi else a_lo), (n - 7) * BANK
            return t[:, c:c + BANK]

        @block.sync
        def _(sp):
            sp.dma_start(xs[0][:, :, :], x[0].rearrange("(j p) d -> p j d", p=P)).then_inc(x_in[0], 16)
            sp.dma_start(wq_in, Wq.rearrange("(h e) c -> e h c", h=H)).then_inc(weights_in, 16)
            sp.dma_start(wk_in, Wk.rearrange("(h e) c -> e h c", h=H)).then_inc(weights_in, 16)
            sp.dma_start(wv_in[:, :, :], Wv.rearrange("(h e) c -> e h c", h=H)).then_inc(weights_in, 16)
            sp.dma_start(wo_in[:, :], Wo).then_inc(weights_in, 16)
            sp.dma_start(wg_in[:, :], Wg).then_inc(weights_in, 16)
            for n, w in enumerate((Wr, Wkf, Wvf)):
                sp.dma_start(ffn_in[:, n, :], w).then_inc(weights_in, 16)
            sp.dma_start(bg_all[:, :], bg.partition_broadcast(P)).then_inc(weights_in, 16)
            sp.dma_start(gain_all[:, :], gain.partition_broadcast(P)).then_inc(weights_in, 16)
            sp.dma_start(mu[:, 0:1], mu_r.rearrange("(p o) -> p o", o=1)).then_inc(weights_in, 16)
            sp.dma_start(mu[:, 1:2], mu_k.rearrange("(p o) -> p o", o=1)).then_inc(weights_in, 16)
            sp.dma_start(xs[1][:, :, :], x[1].rearrange("(j p) d -> p j d", p=P)).then_inc(x_in[1], 16)

            def run(s, par, last):
                known = isinstance(s, int)
                if not (known and s + 2 >= NSEQ):
                    sp.wait_ge(xn_ready, s + 1)
                    sp.dma_start(xs[par][:, :, :], x[s + 2].rearrange("(j p) d -> p j d", p=P))\
                        .then_inc(x_in[par], 16)
                if not (known and s == 0):
                    sp.wait_ge(y_ready, s)
                    sp.dma_start(out[s - 1].rearrange("(j p) d -> p j d", p=P), y[:, :, :]).then_inc(y_out, 16)
                    sp.wait_ge(y_out, s * 16)
                sp.dma_start(y[:, :, :], x[s].rearrange("(j p) d -> p j d", p=P)).then_inc(residual_in, 16)

            sequences(sp, run)
            sp.wait_ge(y_ready, NSEQ)
            sp.dma_start(out[NSEQ - 1].rearrange("(j p) d -> p j d", p=P), y[:, :, :]).then_inc(y_out, 16)
            sp.wait_ge(y_out, 16 * NSEQ)

        NWEIGHTS = 16 * 12

        @block.tensor
        def _(pe):
            pe.wait_ge(weights_in, NWEIGHTS)
            pe.wait_ge(consts_ready, 1)
            pe.wait_ge(pick_ready, 8)
            for n in range(11):
                need(pe, setup_read, n - 1)
                pb = PJ[n % 2]
                if n < 4:
                    w = (wq_in, wk_in)[n // 2]
                    for i in range(HB):
                        last = pe.transpose(pb[:, i * D:(i + 1) * D], w[:, (n % 2) * HB + i, :], ident[:, :])
                elif n < 6:
                    for i in range(HB):
                        h = (n - 4) * HB + i
                        last = pe.transpose(pb[:, i * D:(i + 1) * D], wo_in[:, h * D:(h + 1) * D], ident[:, :])
                elif n == 6:
                    for i in range(3):
                        pe.transpose(pb[:, i * D:(i + 1) * D], ffn_in[:, i, :], ident[:, :])
                    last = pe.transpose(pb[:, 3 * D:3 * D + H], wg_in[:, :], ident[0:H, 0:H])
                elif n < 9:
                    for i in range(HB):
                        h = (n - 7) * HB + i
                        last = pe.matmul(pb[:, i * D:(i + 1) * D], wq_in[:, h, :], wk_in[:, h, :],
                                         start=True, stop=True)
                else:
                    for i in range(HB):
                        h = (n - 9) * HB + i
                        last = pe.matmul(pb[:, i * D:(i + 1) * D], wv_in[:, h, :], woT[:, h, :],
                                         start=True, stop=True)
                last.then_inc(setup_filled, 1)

            def xT_stage(s, par):
                pe.wait_ge(xn_ready, s + 1)
                for j in range(NT):
                    last = pe.transpose(MI[:, j * P:(j + 1) * P], xn[par][:, j, :], ident[:, :])
                last.then_inc(xT_filled, 1)

            def z_stage(s, par):
                pe.wait_ge(xhi_ready, s + 1)
                for j in range(NT):
                    last = pe.matmul(MI[:, j * H:(j + 1) * H], xT[par][:, 1 + j * P:1 + (j + 1) * P],
                                     small_wT[:, 3 * D:3 * D + H], start=True, stop=True)
                last.then_inc(z_filled, 1)

            def gate_stage(s):
                pe.wait_ge(logg_ready, s + 1)
                for kind in range(3):
                    last = pe.matmul(MI[:, kind * NT * H:(kind + 1) * NT * H], span[:, kind, :],
                                     log_g[:, :, :].rearrange("p j h -> p (j h)"), start=True, stop=True)
                last.then_inc(gates_filled, 1)

            def r_stage(s):
                pe.wait_ge(xrk_ready, s + 1)
                pe.matmul(MI[:, :], small_wT[:, 0:D], xr[:, :], start=True, stop=True).then_inc(r_filled, 1)

            def k_stage(s):
                pe.wait_ge(rexp_ready, s + 1)
                pe.matmul(MI[:, :], small_wT[:, D:2 * D], xk[:, :], start=True, stop=True).then_inc(k_filled, 1)

            def v_stage(s):
                pe.wait_ge(kact_ready, s + 1)
                pe.wait_ge(partsT_ready, s * NT + 2)
                pe.matmul(MI[:, :], small_wT[:, 2 * D:3 * D], k_act[:, :], start=True, stop=True)\
                    .then_inc(v_filled, 1)

            def product(n, pb, hi_lo_pairs):
                need(pe, proj_read, n - 1)
                for i, (lhsT, rhs) in enumerate(hi_lo_pairs):
                    last = pe.matmul(pb[:, :], lhsT, rhs, start=(i == 0), stop=(i == len(hi_lo_pairs) - 1))
                last.then_inc(proj_filled, 1)

            def p_stage(s, par, hs, first_job):
                pe.wait_ge(xlo_ready, s + 1)
                for i, h in enumerate(hs):
                    cols = slice(h * D, (h + 1) * D)
                    product(first_job + i, PJ[h % 2], [(a_hi[:, cols], xT_hi[par][:, :]), (a_hi[:, cols], xT_lo[par][:, :]),
                                            (a_lo[:, cols], xT_hi[par][:, :])])

            def project(par, j, first_job, ks):
                t = slice(j * P, (j + 1) * P)
                for i, k in enumerate(ks):
                    cols = slice(k * BANK, (k + 1) * BANK)
                    product(first_job + i, PJ[k % 2], [(xT_hi[par][:, t], w_hi[:, cols]), (xT_hi[par][:, t], w_lo[:, cols]),
                                            (xT_lo[par][:, t], w_hi[:, cols])])

            def spread(dst, j0, b):
                for i in range(HB):
                    last = pe.matmul(dst[:, i * P:(i + 1) * P], pick[:, j0 + i, :], partsT[b % 2][:, :],
                                     start=True, stop=True)
                return last

            def turn(b, g):
                pe.wait_ge(att_a_ready, g + 1)
                pe.wait_ge(att_b_ready, g + 1)
                for half in range(2):
                    for h in range(half * HB, (half + 1) * HB):
                        last = pe.transpose(SC[:, h * P:(h + 1) * P], att[b][:, h, :], ident[:, :])
                    last.then_inc(attT_filled, 1)

            def attend(s, par, j):
                g = s * NT + j
                pe.wait_ge(proj_read, v_jobs(s, j))
                if j == 0:
                    need(pe, y_ready, s)
                for h in range(H):
                    if h % HB == 0:
                        pe.wait_ge(attT_ready, g * 2 + 1 + h // HB)
                    last = pe.matmul(OUT[:, j * P:(j + 1) * P], vp[j % 2][:, h * D:(h + 1) * D],
                                     attT[j % 2][:, h, :], start=(j == 0 and h == 0), stop=(h == H - 1))
                last.then_inc(av_done, 1)

            def cross(s, j, half):
                pe.wait_ge(pdec_ready, s * 6 + 2 * (j - 1) + half + 1)
                for h in range(half * HB, (half + 1) * HB):
                    last = pe.matmul(OUT[:, j * P:(j + 1) * P], state[:, h, :], p_dec[:, h, :],
                                     start=(h == 0), stop=False)
                if half == 1:
                    last.then_inc(cross_done, 1)

            def increment(s, par, j, half):
                pe.wait_ge(vscaled_ready, s * 6 + 2 * j + half + 1)
                pe.matmul(BK[half][:, :], xn[par][:, j, :], v_scaled[:, half * BANK:(half + 1) * BANK],
                          start=True, stop=True).then_inc(incr_filled, 1)

            def finish(s):
                pe.wait_ge(sg_ready, s + 1)
                for j in range(NT):
                    last = pe.transpose(OUT[:, j * P:(j + 1) * P], sgT[:, j * P:(j + 1) * P], ident[:, :])
                last.then_inc(outT_filled, 1)

            pe.wait_ge(setup_read, 11)
            xT_stage(0, 0)
            z_stage(0, 0)
            gate_stage(0)
            p_stage(0, 0, range(H), 0)
            project(0, 0, H, range(6))

            def run(s, par, last_s):
                for j in range(NT):
                    g = s * NT + j
                    nxt = not (last_s and j == NT - 1)
                    np_, nj = (par, j + 1) if j < NT - 1 else (1 - par, 0)
                    if nxt:
                        if j == NT - 1:
                            pe.wait_ge(xlo_ready, s + 2)
                        project(np_, nj, job(s, j, 0), (0,))
                    pe.wait_ge(parts_ready, g + 1)
                    if isinstance(s, int) and s == 0 and j == 0:
                        pe.wait_ge(decay_ready, 1)
                    elif j == 1:
                        pe.wait_ge(krelu_ready, s + 1)
                    elif j == 2:
                        if last_s:
                            pe.wait_ge(ffn_ready, s + 1)
                        else:
                            pe.wait_ge(xhi_ready, s + 2)
                    elif j == 3 and not last_s:
                        pe.wait_ge(decay_ready, s + 2)
                    else:
                        pe.wait_ge(partsT_ready, g)
                    pe.transpose(MI16[:, 0:P], parts[:, :], ident16[:, :]).then_inc(partsT_filled, 1)
                    if nxt:
                        project(np_, nj, job(s, j, 1), (1,))
                    if not (isinstance(s, int) and s == 0 and j == 0):
                        turn((j + 1) % 2, g - 1)
                    pe.wait_ge(partsT_ready, g + 1)
                    for half in range(2):
                        if j > 0:
                            pe.wait_ge(state_ready, s * 6 + 2 * j - 1 + half)
                        spread(BK[half][:, :], half * HB, j).then_inc(qrms_filled, 1)
                    if j > 0:
                        attend(s, par, j - 1)
                    elif not (isinstance(s, int) and s == 0):
                        attend(s - 1, 1 - par, NT - 1)
                    for half in range(2):
                        spread(SC[:, half * BANK:(half + 1) * BANK], H + half * HB, j).then_inc(krms_filled, 1)
                    if j == 1:
                        v_stage(s)
                    if nxt:
                        project(np_, nj, job(s, j, 2), (2,))
                    if j == 2 and not last_s:
                        z_stage(s + 1, 1 - par)
                    if nxt:
                        project(np_, nj, job(s, j, 3), (3,))
                    for half in range(2):
                        pe.wait_ge(krms_ready, g * 2 + half + 1)
                        pe.matmul(SC[:, half * BANK:(half + 1) * BANK], ident16[:, :],
                                  mask[:, :, :].rearrange("p h s -> p (h s)"), start=True, stop=False)
                    for half in range(2):
                        pe.wait_ge(pq_ready, g * 2 + half + 1)
                        for h in range(half * HB, (half + 1) * HB):
                            last = pe.matmul(SC[:, h * P:(h + 1) * P], p_q[j % 2][:, h, :],
                                             xT[par][:, 1 + j * P:1 + (j + 1) * P], start=False,
                                             stop=(h % HB == HB - 1))
                        last.then_inc(scores_filled, 1)
                    makes_p = j >= 2 and not last_s
                    if j == 0:
                        pe.wait_ge(partsT_ready, g + 1)
                        r_stage(s)
                        if not (isinstance(s, int) and s == 0):
                            finish(s - 1)
                    if j == 1 and not last_s:
                        pe.wait_ge(ffn_ready, s + 1)
                        xT_stage(s + 1, 1 - par)
                    for half in range(2):
                        if makes_p:
                            p_stage(s + 1, 1 - par, p_heads(j, half), job(s, j, p_at(half)))
                        if j > 0:
                            cross(s, j, half)
                    for half in range(2):
                        if nxt:
                            project(np_, nj, job(s, j, v_at(s, j) + half), (4 + half,))
                        if j < NT - 1:
                            increment(s, par, j, half)
                        if j == 0 and half == 0:
                            k_stage(s)
                    if makes_p:
                        p_stage(s + 1, 1 - par, p_heads(j, 2), job(s, j, p_at(2)))
                        if j == 2:
                            gate_stage(s + 1)
                        p_stage(s + 1, 1 - par, p_heads(j, 3), job(s, j, p_at(3)))

            sequences(pe, run)
            turn(1, NSEQ * NT - 1)
            attend(NSEQ - 1, 1, NT - 1)
            finish(NSEQ - 1)

        @block.scalar
        def _(act):
            for n in SPLIT_JOBS:
                act.wait_ge(setup_filled, n + 1)
                act.activation(split_dst(n, True), PJ[n % 2][:, :], ACT.Copy).then_inc(setup_hi, 1)

            def norm_stage(s):
                act.wait_ge(var_ready, s + 1)
                act.activation(ln_var[:, :], mean_var[:, :, 1], ACT.Ln, bias=eps[:, 0:1]).then_inc(lnvar_done, 1)
                act.wait_ge(lnvar_done, s + 1)
                act.activation(rstd[:, :], ln_var[:, :], ACT.Exp, scale=-0.5).then_inc(rstd_ready, 1)

            def xT_stage(s, par):
                act.wait_ge(xT_filled, s + 1)
                act.activation(xT[par][:, 1:1 + T], MI[:, :], ACT.Copy).then_inc(xT_ready, 1)
                act.activation(xT_hi[par][:, :], MI[:, :], ACT.Copy).then_inc(xhi_ready, 1)

            def mix_stage(s, par):
                act.wait_ge(xT_ready, s + 1)
                act.wait_ge(small_ready, 2)
                need(act, xrk_ready, s)
                act.activation(mix_r[:, :], xT[par][:, 0:T], ACT.Copy, scale=one_minus_mu[:, 0:1]).then_inc(mix_ready, 1)
                act.activation(mix_k[:, :], xT[par][:, 0:T], ACT.Copy, scale=one_minus_mu[:, 1:2]).then_inc(mix_ready, 1)

            def gate_log_stage(s):
                act.wait_ge(zneg_ready, s + 1)
                act.activation(z_l1p[:, :, :], z_neg[:, :, :], ACT.Exp).then_inc(zexp_done, 1)
                act.wait_ge(zexp_done, s + 1)
                act.activation(z_l1p[:, :, :], z_l1p[:, :, :], ACT.Ln, bias=1.0).then_inc(zl1p_ready, 1)

            def decay_stage(s, par):
                act.wait_ge(gates_filled, s + 1)
                n = NT * H
                act.activation(q_decay[par][:, :, :, 1], MI[:, 0:n].rearrange("p (j h) -> p j h", j=NT), ACT.Exp)
                act.activation(decay[par][:, :, :, :].rearrange("p k j h -> p (k j h)"), MI[:, n:3 * n], ACT.Exp)\
                    .then_inc(decay_ready, 1)

            def r_stage(s):
                act.wait_ge(r_filled, s + 1)
                need(act, rone_done, s)
                act.activation(r_exp[:, :], MI[:, :], ACT.Exp, scale=-1.0).then_inc(rexp_ready, 1)

            def k_stage(s):
                act.wait_ge(k_filled, s + 1)
                act.activation(k_relu[:, :], MI[:, :], ACT.Relu).then_inc(krelu_ready, 1)
                act.wait_ge(krelu_ready, s + 1)
                need(act, v_filled, s)
                act.activation(k_act[:, :], k_relu[:, :], ACT.Square).then_inc(kact_ready, 1)

            def f_stage(s):
                act.wait_ge(ffn_ready, s + 1)
                act.activation(f_exp[:, :], ffn[:, :], ACT.Exp, scale=-1.0).then_inc(fexp_ready, 1)

            def p_stage(s, par, hs, first_job):
                for i, h in enumerate(hs):
                    act.wait_ge(proj_filled, first_job + i + 1)
                    act.activation(p_raw[par][:, h, :], PJ[h % 2][:, :], ACT.Copy).then_inc(proj_read, 1)

            def squares(b, first_job, k):
                act.wait_ge(proj_filled, first_job + k + 1)
                for i in range(HB):
                    last = act.activation(squared[:, k * HB + i, :], PJ[k % 2][:, i * D:(i + 1) * D], ACT.Square,
                                          accum_out=ssq[b][:, k * HB + i:k * HB + i + 1])
                last.then_inc(proj_read, 1)

            def rms_stage(b, first_job, count):
                act.wait_ge(proj_read, first_job + 4)
                act.activation(ln_ms[:, :], ssq[b][:, :], ACT.Ln, bias=eps[:, 1:2], scale=1.0 / DK)\
                    .then_inc(lnms_done, 1)
                act.wait_ge(lnms_done, count)
                act.activation(rms[b][:, :], ln_ms[:, :], ACT.Exp, scale=-0.5).then_inc(rms_ready, 1)

            def v_stage(b, first_job, i, tiles_done):
                need(act, av_done, tiles_done)
                act.wait_ge(proj_filled, first_job + i + 1)
                act.activation(vp[b][:, i * BANK:(i + 1) * BANK], PJ[i][:, :], ACT.Copy).then_inc(proj_read, 1)

            act.preload_act_table_set("natural_log_exp_and_others")
            act.wait_ge(small_ready, 2)
            norm_stage(0)
            xT_stage(0, 0)
            mix_stage(0, 0)
            gate_log_stage(0)
            decay_stage(0, 0)
            p_stage(0, 0, range(H), 0)
            for k in range(4):
                squares(0, H, k)
            rms_stage(0, H, 1)
            for i in range(2):
                v_stage(0, H + 4, i, 0)

            def attT_stage(b, g):
                for half in range(2):
                    act.wait_ge(attT_filled, g * 2 + half + 1)
                    act.activation(attT[b][:, half * HB:(half + 1) * HB, :],
                                   SCh[:, half * HB:(half + 1) * HB, :], ACT.Copy).then_inc(attT_ready, 1)

            def run(s, par, last_s):
                for j in range(NT):
                    g = s * NT + j
                    nxt = not (last_s and j == NT - 1)
                    nb = (j + 1) % 2
                    if nxt:
                        squares(nb, job(s, j, 0), 0)
                    if not (isinstance(s, int) and s == 0 and j == 0):
                        attT_stage(nb, g - 1)
                    if nxt:
                        squares(nb, job(s, j, 0), 1)
                    for half in range(2):
                        act.wait_ge(krms_filled, g * 2 + half + 1)
                        act.activation(k_rms[j % 2][:, half * BANK:(half + 1) * BANK],
                                       SC[:, half * BANK:(half + 1) * BANK], ACT.Copy).then_inc(krms_ready, 1)
                    if nxt:
                        squares(nb, job(s, j, 0), 2)
                    if j == 0 and not last_s:
                        norm_stage(s + 1)
                    if j == 2 and not last_s:
                        mix_stage(s + 1, 1 - par)
                    if nxt:
                        squares(nb, job(s, j, 0), 3)
                    if j == 2 and not last_s:
                        gate_log_stage(s + 1)
                    if nxt:
                        rms_stage(nb, job(s, j, 0), g + 2)
                    makes_p = j >= 2 and not last_s
                    if j == 0:
                        r_stage(s)
                    if j == 1 and not last_s:
                        xT_stage(s + 1, 1 - par)
                    if makes_p:
                        for i in range(2):
                            p_stage(s + 1, 1 - par, p_heads(j, i), job(s, j, p_at(i)))
                    if j == 0:
                        v_stage(nb, job(s, j, v_at(s, j)), 0, g)
                    act.wait_ge(shifted_ready, g + 1)
                    act.activation(own[j % 2][:, :, :], own[j % 2][:, :, :], ACT.Exp, scale=SCALE)\
                        .then_inc(exp_ready, 1)
                    if j == 0:
                        k_stage(s)
                    if nxt:
                        for i in range(1 if j == 0 else 0, 2):
                            v_stage(nb, job(s, j, v_at(s, j)), i, g)
                    if j == 1:
                        f_stage(s)
                    if makes_p:
                        p_stage(s + 1, 1 - par, p_heads(j, 2), job(s, j, p_at(2)))
                        if j == 2:
                            decay_stage(s + 1, 1 - par)
                        p_stage(s + 1, 1 - par, p_heads(j, 3), job(s, j, p_at(3)))

            sequences(act, run)
            attT_stage(1, NSEQ * NT - 1)

        @block.vector
        def _(dve):
            dve.memset(eps[:, 0:1], LN_EPS)
            dve.memset(eps[:, 1:2], RMS_EPS).then_inc(small_ready, 1)
            dve.memset(parts[:, :], 0.0)
            for b in range(2):
                dve.memset(xT[b][:, 0:1], 0.0)
                dve.memset(att[b][:, :, :], 0.0)
                dve.memset(q_decay[b][:, :, :, 0], 1.0)
            dve.memset(span[:, :, :], 0.0).then_inc(zeroed, 1)
            dve.wait_ge(zeroed, 1)
            dve.memset(span[0:CH, 0, :], 1.0)
            dve.memset(span[:, 1, :], 1.0)
            dve.memset(span[CH:P, 2, 0:CH], 1.0).then_inc(consts_ready, 1)
            dve.wait_ge(weights_in, NWEIGHTS)
            dve.tensor_scalar(one_minus_mu[:, :], mu[:, :], -1.0, 1.0, ALU.mult, ALU.add).then_inc(small_ready, 1)

            def norm_stats(s, par, loads):
                dve.wait_ge(x_in[par], loads)
                for j in range(NT):
                    last = dve.bn_stats(stats[:, j, :], xs[par][:, j, :])
                last.then_inc(stats_done, 1)
                dve.wait_ge(stats_done, s + 1)
                dve.memset(scratch[:, :], 0.0)
                for j in range(NT):
                    last = dve.bn_aggr(mean_var[:, j, :], stats[:, j, :])
                last.then_inc(var_ready, 1)

            def norm_stage(s, par):
                dve.wait_ge(var_ready, s + 1)
                dve.wait_ge(rstd_ready, s + 1)
                for j in range(NT):
                    last = dve.tensor_scalar(xn[par][:, j, :], xs[par][:, j, :], mean_var[:, j, 0:1],
                                             rstd[:, j:j + 1], ALU.subtract, ALU.mult)
                last.then_inc(xn_ready, 1)

            def xlo_stage(s, par):
                dve.wait_ge(xhi_ready, s + 1)
                dve.tensor_tensor(xT_lo[par][:, :], xT[par][:, 1:1 + T], xT_hi[par][:, :].bitcast(F32),
                                  ALU.subtract).then_inc(xlo_ready, 1)

            def mix_stage(s, par):
                dve.wait_ge(mix_ready, s * 2 + 2)
                need(dve, k_filled, s)
                dve.scalar_tensor_tensor(xr[:, :], xT[par][:, 1:1 + T], mu[:, 0:1], mix_r[:, :], ALU.mult, ALU.add)
                dve.scalar_tensor_tensor(xk[:, :], xT[par][:, 1:1 + T], mu[:, 1:2], mix_k[:, :], ALU.mult, ALU.add)\
                    .then_inc(xrk_ready, 1)

            def z_stage(s):
                dve.wait_ge(z_filled, s + 1)
                dve.tensor_tensor(zb[:, :, :], MI[:, 0:NT * H].rearrange("p (j h) -> p j h", j=NT),
                                  bg_all[:, :].rearrange("p (o h) -> p o h", o=1).broadcast_to([P, NT, H]), ALU.add)\
                    .then_inc(zb_done, 1)
                dve.wait_ge(zb_done, s + 1)
                dve.scalar_tensor_tensor(z_neg[:, :, :], zb[:, :, :], -1.0, zb[:, :, :], ALU.mult, ALU.min)\
                    .then_inc(zneg_ready, 1)

            def gate_stage(s):
                dve.wait_ge(zl1p_ready, s + 1)
                dve.scalar_tensor_tensor(log_g[:, :, :], zb[:, :, :], 0.0, z_l1p[:, :, :], ALU.min, ALU.subtract)\
                    .then_inc(logg_ready, 1)

            HALF = T // 2

            def r_stage(s, half):
                if half == 0:
                    dve.wait_ge(rexp_ready, s + 1)
                    need(dve, ffn_ready, s)
                    dve.tensor_scalar(r_sig[:, :], r_exp[:, :], 1.0, None, ALU.add).then_inc(rone_done, 1)
                    dve.wait_ge(rone_done, s + 1)
                t = slice(half * HALF, (half + 1) * HALF)
                dve.reciprocal(r_sig[:, t], r_sig[:, t]).then_inc(rsig_done, 1)

            def v_stage(s):
                dve.wait_ge(v_filled, s + 1)
                dve.wait_ge(rsig_done, s * 2 + 2)
                dve.tensor_tensor(ffn[:, :], MI[:, :], r_sig[:, :], ALU.mult).then_inc(ffn_ready, 1)

            def f_stage(s, half):
                if half == 0:
                    dve.wait_ge(fexp_ready, s + 1)
                    dve.tensor_scalar(f_exp[:, :], f_exp[:, :], 1.0, None, ALU.add).then_inc(fone_done, 1)
                    dve.wait_ge(fone_done, s + 1)
                t = slice(half * HALF, (half + 1) * HALF)
                dve.reciprocal(f_exp[:, t], f_exp[:, t]).then_inc(fsig_done, 1)

            def silu_stage(s, par):
                dve.wait_ge(fsig_done, s * 2 + 2)
                dve.tensor_tensor(gT[par][:, :], ffn[:, :], f_exp[:, :], ALU.mult).then_inc(gT_ready, 1)

            def split_factors(step, b, count):
                if step == 0:
                    dve.wait_ge(rms_ready, count)
                    dve.tensor_scalar(rms[b][:, 0:H], rms[b][:, 0:H], gain_all[:, 0:1], None, ALU.mult)\
                        .then_inc(gained, 1)
                elif step == 1:
                    dve.wait_ge(gained, count)
                    need(dve, partsT_filled, count - 1)
                    dve.tensor_copy(parts[:, 0:NR], rms[b][:, :]).then_inc(split_step, 1)
                elif step == 2:
                    dve.wait_ge(split_step, count * 4 - 3)
                    dve.tensor_tensor(res1[:, :], rms[b][:, :], parts[:, 0:NR], ALU.subtract).then_inc(split_step, 1)
                elif step == 3:
                    dve.wait_ge(split_step, count * 4 - 2)
                    dve.tensor_copy(parts[:, NR:2 * NR], res1[:, :]).then_inc(split_step, 1)
                elif step == 4:
                    dve.wait_ge(split_step, count * 4 - 1)
                    dve.tensor_tensor(res2[:, :], res1[:, :], parts[:, NR:2 * NR], ALU.subtract)\
                        .then_inc(split_step, 1)
                else:
                    dve.wait_ge(split_step, count * 4)
                    dve.tensor_copy(parts[:, 2 * NR:3 * NR], res2[:, :]).then_inc(parts_ready, 1)

            def partsT_stage(b, count):
                dve.wait_ge(partsT_filled, count)
                dve.tensor_copy(partsT[b][:, :], MI16[:, 0:P]).then_inc(partsT_ready, 1)

            def state_update(s, par, j, half):
                if half == 0:
                    dve.wait_ge(decay_ready, s + 1)
                    if j > 0:
                        dve.wait_ge(state_ready, s * 6 + 2 * j)
                dve.wait_ge(incr_filled, s * 6 + 2 * j + half + 1)
                if j == 0:
                    last = dve.tensor_copy(state[:, half * HB:(half + 1) * HB, :].rearrange("p h d -> p (h d)"),
                                           BK[half][:, :])
                else:
                    for i in range(HB):
                        h = half * HB + i
                        last = dve.scalar_tensor_tensor(
                            state[:, h, :], state[:, h, :], decay[par][:, 0, j, h:h + 1],
                            BK[half][:, i * D:(i + 1) * D], ALU.mult, ALU.add)
                last.then_inc(state_ready, 1)

            y_flat = y[:, :, :].rearrange("p j d -> p (j d)")
            norm_stats(0, 0, 16)
            for n in range(11):
                dve.wait_ge(setup_filled, n + 1)
                if n in SPLIT_JOBS:
                    dve.wait_ge(setup_hi, SPLIT_JOBS.index(n) + 1)
                    last = dve.tensor_tensor(split_dst(n, False), PJ[n % 2][:, :], split_dst(n, True).bitcast(F32),
                                             ALU.subtract)
                elif n < 6:
                    last = dve.tensor_copy(woT[:, (n - 4) * HB:(n - 3) * HB, :].rearrange("p h d -> p (h d)"),
                                           PJ[n % 2][:, :])
                else:
                    last = dve.tensor_copy(small_wT[:, :], PJ[n % 2][:, 0:3 * D + H])
                last.then_inc(setup_read, 1)
            norm_stage(0, 0)
            xlo_stage(0, 0)
            z_stage(0)
            gate_stage(0)
            mix_stage(0, 0)
            for step in range(6):
                split_factors(step, 0, 1)
            partsT_stage(0, 1)

            def run(s, par, last_s):
                first = isinstance(s, int) and s == 0
                for j in range(NT):
                    g = s * NT + j
                    b = j % 2
                    nxt = not (last_s and j == NT - 1)
                    if j == 0:
                        dve.wait_ge(proj_read, H if first else job(s - 1, NT - 1, p_at(3)) + 1)
                    for half in range(2):
                        dve.wait_ge(qrms_filled, g * 2 + half + 1)
                        hs = slice(half * HB, (half + 1) * HB)
                        dve.tensor_tensor(p_q[b][:, hs, :], p_raw[par][:, hs, j * P:(j + 1) * P],
                                          BK[half][:, :].rearrange("p (h t) -> p h t", h=HB), ALU.mult)\
                            .then_inc(pq_ready, 1)
                    if j == 0 and not first:
                        dve.wait_ge(av_done, g)
                        dve.wait_ge(gT_ready, s)
                        dve.tensor_tensor(sgT[:, :], OUT[:, :], gT[1 - par][:, :], ALU.mult).then_inc(sg_ready, 1)
                    if j == 0:
                        if not last_s:
                            norm_stats(s + 1, 1 - par, x_loads(s, par))
                    if j == 1:
                        if not last_s:
                            norm_stage(s + 1, 1 - par)
                        r_stage(s, 1)
                        v_stage(s)
                    if j == 2:
                        if not last_s:
                            xlo_stage(s + 1, 1 - par)
                            z_stage(s + 1)
                        f_stage(s, 0)
                    if j == 3:
                        if not last_s:
                            mix_stage(s + 1, 1 - par)
                        f_stage(s, 1)
                    dve.wait_ge(krms_ready, g * 2 + 2)
                    dve.wait_ge(scores_filled, g * 2 + 2)
                    kr = k_rms[b][:, :].rearrange("p (h s) -> p h s", h=H)
                    if nxt:
                        split_factors(0, (j + 1) % 2, g + 2)
                    dve.tensor_tensor(own[b][0:CH, :, :], SCh[0:CH, :, 0:CH], kr[0:CH, :, 0:CH], ALU.mult)
                    if nxt:
                        split_factors(1, (j + 1) % 2, g + 2)
                    dve.tensor_tensor(own[b][CH:P, :, :], SCh[CH:P, :, CH:P], kr[CH:P, :, CH:P], ALU.mult)\
                        .then_inc(own_ready, 1)
                    if nxt:
                        split_factors(2, (j + 1) % 2, g + 2)
                    dve.wait_ge(own_ready, g + 1)
                    dve.tensor_reduce(top[:, :], own[b][:, :, :], AX.X, ALU.max).then_inc(top_done, 1)
                    if nxt:
                        split_factors(3, (j + 1) % 2, g + 2)
                    dve.wait_ge(top_done, g + 1)
                    dve.tensor_tensor(own[b][:, :, :], own[b][:, :, :], over(top), ALU.subtract)\
                        .then_inc(shifted_ready, 1)
                    if nxt:
                        split_factors(4, (j + 1) % 2, g + 2)
                    dve.tensor_tensor(att[b][CH:P, :, 0:CH], SCh[CH:P, :, 0:CH], kr[CH:P, :, 0:CH], ALU.mult)
                    if j == 2 and not last_s:
                        gate_stage(s + 1)
                    if nxt:
                        split_factors(5, (j + 1) % 2, g + 2)
                    dve.wait_ge(exp_ready, g + 1)
                    dve.tensor_reduce(total[:, :], own[b][:, :, :], AX.X, ALU.add).then_inc(total_done, 1)
                    dve.wait_ge(total_done, g + 1)
                    dve.reciprocal(inv_total[b][:, :], total[:, :]).then_inc(inv_ready, 1)
                    dve.wait_ge(inv_ready, g + 1)
                    dve.tensor_tensor(att[b][0:CH, :, 0:CH], own[b][0:CH, :, :], over(inv_total[b])[0:CH, :, :],
                                      ALU.mult).then_inc(att_a_ready, 1)
                    if j < NT - 1:
                        state_update(s, par, j, 0)
                    if nxt:
                        partsT_stage((j + 1) % 2, g + 2)
                    if j < NT - 1:
                        state_update(s, par, j, 1)
                    if j == 0 and not first:
                        dve.wait_ge(outT_filled, s)
                        dve.wait_ge(residual_in, s * 16)
                        dve.tensor_tensor(y_flat, OUT[:, :], y_flat, ALU.add)\
                            .then_inc(y_ready, 1)
                    if j == 0:
                        r_stage(s, 0)
                    if j == 3:
                        silu_stage(s, par)

            def x_loads(s, par):
                return s * 8 + (16 if par == 0 else 24)

            def over(v):
                return v[:, :].rearrange("p (h o) -> p h o", o=1).broadcast_to([P, H, CH])

            sequences(dve, run)
            dve.wait_ge(av_done, NSEQ * NT)
            dve.wait_ge(gT_ready, NSEQ)
            dve.tensor_tensor(sgT[:, :], OUT[:, :], gT[1][:, :], ALU.mult).then_inc(sg_ready, 1)
            dve.wait_ge(outT_filled, NSEQ)
            dve.wait_ge(residual_in, 16 * NSEQ)
            dve.tensor_tensor(y_flat, OUT[:, :], y_flat, ALU.add).then_inc(y_ready, 1)

        @block.gpsimd
        def _(pool):
            pool.memset(ident[:, :], 0.0)
            pool.memset(ident16[:, :], 0.0)
            pool.memset(mask[:, :, :], 0.0)
            pool.memset(pick[:, :, :], 0.0).then_inc(pick_ready, 1)
            pool.wait_ge(pick_ready, 1)
            for m in (ident, ident16):
                pool.affine_select(out=m[:, :], in_=m[:, :], compare_op=ALU.not_equal, fill=1.0, base=0,
                                   pattern=[[-1, P]], channel_multiplier=1).then_inc(pick_ready, 1)
            for a in range(2):
                pool.wait_ge(pick_ready, 3 + a)
                rows = mask[a * CH:(a + 1) * CH, :, a * CH:(a + 1) * CH]
                pool.affine_select(out=rows, in_=rows, compare_op=ALU.is_ge, fill=MASKED, base=0,
                                   pattern=[[0, HB], [-1, CH]], channel_multiplier=1).then_inc(pick_ready, 1)
            for part in range(3):
                pool.wait_ge(pick_ready, part + 5)
                pool.affine_select(out=pick[:, :, :], in_=pick[:, :, :], compare_op=ALU.not_equal, fill=1.0,
                                   base=-part * NR, pattern=[[-1, NR], [0, P]], channel_multiplier=1)\
                    .then_inc(pick_ready, 1)

            def run(s, par, last_s):
                for j in range(NT):
                    g = s * NT + j
                    b = j % 2
                    if j == 0:
                        pool.wait_ge(decay_ready, s + 1)
                    need(pool, att_b_ready, g)
                    if j < NT - 1:
                        pool.wait_ge(rms_ready, g + 1)
                        need(pool, incr_filled, s * 6 + 2 * j)
                        pool.tensor_tensor(v_scale[:, :], rms[b][:, H:NR], decay[par][:, 1, j, :], ALU.mult)\
                            .then_inc(vscale_done, 1)
                        pool.wait_ge(vscale_done, s * 3 + j + 1)
                        pool.wait_ge(proj_read, v_jobs(s, j))
                        for half in range(2):
                            hs = slice(half * HB, (half + 1) * HB)
                            cs = slice(half * BANK, (half + 1) * BANK)
                            pool.tensor_tensor(
                                v_scaled[:, cs].rearrange("p (h d) -> p h d", h=HB),
                                vp[b][:, cs].rearrange("p (h d) -> p h d", h=HB),
                                v_scale[:, hs].rearrange("p (h o) -> p h o", o=1).broadcast_to([P, HB, D]),
                                ALU.mult).then_inc(vscaled_ready, 1)
                    if j > 0:
                        need(pool, cross_done, s * 3 + j - 1)
                        for half in range(2):
                            pool.wait_ge(pq_ready, g * 2 + half + 1)
                            hs = slice(half * HB, (half + 1) * HB)
                            pool.tensor_tensor(
                                p_dec[:, hs, :].rearrange("p h (a t) -> p (h a) t", a=2),
                                p_q[b][:, hs, :].rearrange("p h (a t) -> p (h a) t", a=2),
                                q_decay[par][:, j, hs, :].rearrange("p h (a o) -> p (h a) o", o=1)
                                .broadcast_to([P, 2 * HB, CH]), ALU.mult).then_inc(pdec_ready, 1)
                    if j > 0:
                        pool.wait_ge(pdec_ready, s * 6 + 2 * j)
                    else:
                        pool.wait_ge(vscaled_ready, s * 6 + 2)
                    pool.wait_ge(inv_ready, g + 1)
                    pool.tensor_tensor(att[b][CH:P, :, CH:P], own[b][CH:P, :, :],
                                       inv_total[b][CH:P, :].rearrange("p (h o) -> p h o", o=1)
                                       .broadcast_to([CH, H, CH]), ALU.mult).then_inc(att_b_ready, 1)

            sequences(pool, run)


_INS = ["x", "Wq", "Wk", "Wv", "Wg", "bg", "Wo", "gain", "Wr", "Wkf", "Wvf", "mu_r", "mu_k"]


def kernel(L0_attn_x, L0_attn_Wq, L0_attn_Wk, L0_attn_Wv, L0_attn_Wg, L0_attn_bg, L0_attn_Wo, L0_attn_qk_gain,
           L0_ffn_W_r, L0_ffn_W_k, L0_ffn_W_v, L0_ffn_mu_r, L0_ffn_mu_k):
    import concourse.bacc as bacc
    from concourse.bass_utils import run_bass_kernel_spmd

    values = [L0_attn_x, L0_attn_Wq, L0_attn_Wk, L0_attn_Wv, L0_attn_Wg, L0_attn_bg, L0_attn_Wo,
              np.asarray(L0_attn_qk_gain).reshape(1), L0_ffn_W_r, L0_ffn_W_k, L0_ffn_W_v, L0_ffn_mu_r, L0_ffn_mu_k]
    nc = bacc.Bacc("TRN2", target_bir_lowering=False, num_devices=1)
    arrays, args = {}, []
    for name, value in zip(_INS, values):
        a = np.ascontiguousarray(value)
        arrays[f"in_{name}"] = a
        args.append(nc.dram_tensor(f"in_{name}", a.shape, mybir.dt.from_np(a.dtype), kind="ExternalInput").ap())
    shape = arrays["in_x"].shape
    args.append(nc.dram_tensor("out", shape, F32, kind="ExternalOutput").ap())
    build(nc, *args)
    r = run_bass_kernel_spmd(nc, [arrays], core_ids=[0])
    return r.results[0]["out"]
```

```python
from contextlib import ExitStack

import numpy as np
import concourse.bass as bass
from concourse import mybir

F32 = mybir.dt.float32
F32R = mybir.dt.float32r
BF16 = mybir.dt.bfloat16
ALU = mybir.AluOpType
ACT = mybir.ActivationFunctionType
AX = mybir.AxisListType

P = 128
CH = 64
BANK = 512
MASKED = -1.0e30
LN_EPS = 1.0e-5
RMS_EPS = 1.0e-6


def build(nc, x, Wq, Wk, Wv, Wg, bg, Wo, gain, Wr, Wkf, Wvf, mu_r, mu_k, out):
    NSEQ, T, D = x.shape
    H = Wg.shape[0]
    DK = Wq.shape[0] // H
    NT = T // P
    HW = H * D
    HB = BANK // D
    assert D == P and DK == P and T == BANK and H == 2 * HB and NT == 4 and NSEQ % 2 == 0
    SCALE = 1.0 / float(np.sqrt(DK))
    NR = 2 * H

    with ExitStack() as ctx:
        def sb(name, shape, dt=F32):
            return ctx.enter_context(nc.sbuf_tensor(name, shape, dt))

        def pair(name, shape, dt=F32):
            return [sb(f"{name}{i}", shape, dt) for i in range(2)]

        def bank(name, n=1):
            return ctx.enter_context(nc.psum_tensor(name, [P, n * BANK], F32))

        def sem(name):
            return ctx.enter_context(nc.semaphore(name))

        wqk_in = sb("wqk_in", [P, 2 * H, D])
        wq_in, wk_in = wqk_in[:, 0:H, :], wqk_in[:, H:2 * H, :]
        wv_in = sb("wv_in", [P, H, D])
        wo_in = sb("wo_in", [P, HW])
        wg_in = sb("wg_in", [H, D])
        ffn_in = sb("ffn_in", [P, 3, D])
        bg_all = sb("bg_all", [P, H])
        gain_all = sb("gain_all", [P, 1])
        mu = sb("mu", [P, 2])
        one_minus_mu = sb("one_minus_mu", [P, 2])
        eps = sb("eps", [P, 2])
        ones = sb("ones", [P, 1])
        scratch = sb("scratch", [P, 1])
        mask = sb("mask", [P, CH])
        mask16 = sb("mask16", [P, HB, P], BF16)
        ident = sb("ident", [P, P])
        ident16 = sb("ident16", [P, P], BF16)
        pick = sb("pick", [P, NR, P], BF16)
        span = sb("span", [P, 3, P])
        woT = sb("woT", [P, H, D])
        small_wT = sb("small_wT", [P, 3 * D + H])
        w_hi = sb("w_hi", [P, 3 * HW], F32R)
        w_lo = sb("w_lo", [P, 3 * HW], F32R)
        a_hi = sb("a_hi", [P, HW], F32R)
        a_lo = sb("a_lo", [P, HW], F32R)
        xs = pair("xs", [P, NT, D])
        stats = sb("stats", [P, NT, 6])
        mean_var = sb("mean_var", [P, NT, 2])
        ln_var = sb("ln_var", [P, NT])
        rstd = sb("rstd", [P, NT])
        xn = pair("xn", [P, NT, D])
        xn_hi = sb("xn_hi", [P, NT, D], F32R)
        xn_lo = sb("xn_lo", [P, NT, D], F32R)
        xT = pair("xT", [P, 1 + T])
        xT_hi = pair("xT_hi", [P, T], F32R)
        xT_lo = pair("xT_lo", [P, T], F32R)
        p_raw = pair("p_raw", [P, H, T])
        mix_r = sb("mix_r", [P, T])
        mix_k = sb("mix_k", [P, T])
        xr = sb("xr", [P, T])
        xk = sb("xk", [P, T])
        r_exp = sb("r_exp", [P, T])
        r_sig = sb("r_sig", [P, T])
        k_relu = sb("k_relu", [P, T])
        k_act = sb("k_act", [P, T])
        ffn = sb("ffn", [P, T])
        f_exp = sb("f_exp", [P, T])
        gT = pair("gT", [P, T])
        zb = sb("zb", [P, NT, H])
        z_neg = sb("z_neg", [P, NT, H])
        z_l1p = sb("z_l1p", [P, NT, H])
        log_g = sb("log_g", [P, NT, H])
        decay = pair("decay", [P, 2, NT, H])
        q_decay = pair("q_decay", [P, NT, H, 2])
        sgT = sb("sgT", [P, T])
        y = sb("y", [P, NT, D])
        squared = wqk_in
        ssq = pair("ssq", [P, NR])
        ln_ms = sb("ln_ms", [P, NR])
        rms = pair("rms", [P, NR])
        res1 = sb("res1", [P, NR])
        res2 = sb("res2", [P, NR])
        parts = sb("parts", [P, P], BF16)
        partsT = pair("partsT", [P, P], BF16)
        vp = pair("vp", [P, HW])
        v_scale = sb("v_scale", [P, H])
        v_scaled = wv_in[:, :, :].rearrange("p h d -> p (h d)")
        v_hi = sb("v_hi", [P, HW], F32R)
        v_lo = sb("v_lo", [P, HW], F32R)
        k_rms = pair("k_rms", [P, HW])
        p_q = pair("p_q", [P, H, P])
        p_dec = wo_in[:, :].rearrange("p (h d) -> p h d", h=H)
        own = pair("own", [P, H, CH])
        top = sb("top", [P, H])
        total = sb("total", [P, H])
        inv_total = pair("inv_total", [P, H])
        att = pair("att", [P, H, P])
        attT = pair("attT", [P, H, P])
        state = woT

        PJ = [bank("PJ0"), bank("PJ1")]
        SC = bank("SC", 2)
        BK = [bank("BK0"), bank("BK1")]
        OUT = bank("OUT")
        MI = bank("MI")
        SCh = SC[:, :].rearrange("p (h s) -> p h s", h=H)
        MI16 = MI[:, :].bitcast(BF16)

        wq_loaded = sem("wq_loaded")
        wk_loaded = sem("wk_loaded")
        wo_loaded = sem("wo_loaded")
        wv_loaded = sem("wv_loaded")
        small_loaded = sem("small_loaded")
        x_in = [sem("x_in0"), sem("x_in1")]
        residual_in = sem("residual_in")
        y_out = sem("y_out")
        zeroed = sem("zeroed")
        consts_ready = sem("consts_ready")
        ident_ready = sem("ident_ready")
        pick_ready = sem("pick_ready")
        small_ready = sem("small_ready")
        setup_filled = sem("setup_filled")
        setup_hi = sem("setup_hi")
        setup_read = sem("setup_read")
        stats_done = sem("stats_done")
        var_ready = sem("var_ready")
        lnvar_done = sem("lnvar_done")
        rstd_ready = sem("rstd_ready")
        xn_ready = sem("xn_ready")
        xT_filled = sem("xT_filled")
        xT_ready = sem("xT_ready")
        xhi_ready = sem("xhi_ready")
        xlo_ready = sem("xlo_ready")
        z_filled = sem("z_filled")
        zb_done = sem("zb_done")
        zneg_ready = sem("zneg_ready")
        zexp_done = sem("zexp_done")
        zl1p_ready = sem("zl1p_ready")
        logg_ready = sem("logg_ready")
        gates_filled = sem("gates_filled")
        decay_ready = sem("decay_ready")
        mix_ready = sem("mix_ready")
        xrk_ready = sem("xrk_ready")
        r_filled = sem("r_filled")
        rexp_ready = sem("rexp_ready")
        k_filled = sem("k_filled")
        krelu_ready = sem("krelu_ready")
        kact_ready = sem("kact_ready")
        rone_done = sem("rone_done")
        rsig_done = sem("rsig_done")
        v_filled = sem("v_filled")
        ffn_ready = sem("ffn_ready")
        fexp_ready = sem("fexp_ready")
        fone_done = sem("fone_done")
        fsig_done = sem("fsig_done")
        gT_ready = sem("gT_ready")
        proj_filled = sem("proj_filled")
        proj_read = sem("proj_read")
        lnms_done = sem("lnms_done")
        rms_ready = sem("rms_ready")
        gained = sem("gained")
        split_step = sem("split_step")
        parts_ready = sem("parts_ready")
        partsT_filled = sem("partsT_filled")
        partsT_ready = sem("partsT_ready")
        krms_filled = sem("krms_filled")
        krms_ready = sem("krms_ready")
        qrms_filled = sem("qrms_filled")
        pq_ready = sem("pq_ready")
        vscale_done = sem("vscale_done")
        vscaled_ready = sem("vscaled_ready")
        vhi_ready = sem("vhi_ready")
        vlo_ready = sem("vlo_ready")
        xnhi_ready = sem("xnhi_ready")
        xnlo_ready = sem("xnlo_ready")
        pdec_ready = sem("pdec_ready")
        scores_filled = sem("scores_filled")
        own_ready = sem("own_ready")
        mask_ready = sem("mask_ready")
        top_done = sem("top_done")
        shifted_ready = sem("shifted_ready")
        exp_ready = sem("exp_ready")
        total_done = sem("total_done")
        inv_ready = sem("inv_ready")
        att_a_ready = sem("att_a_ready")
        att_b_ready = sem("att_b_ready")
        attT_filled = sem("attT_filled")
        attT_ready = sem("attT_ready")
        cross_done = sem("cross_done")
        av_done = sem("av_done")
        incr_filled = sem("incr_filled")
        state_decayed = sem("state_decayed")
        state_ready = sem("state_ready")
        sg_ready = sem("sg_ready")
        outT_filled = sem("outT_filled")
        y_ready = sem("y_ready")

        block = ctx.enter_context(nc.Block())

        def need(eng, s, n):
            if not (isinstance(n, int) and n <= 0):
                eng.wait_ge(s, n)

        def job(s, j, k):
            return H + 6 + s * 32 + (0, 6, 12, 22)[j] + k

        def v_at(s, j):
            return 4 if j < 2 or (isinstance(s, int) and s == NSEQ - 1) else 6

        def p_at(i):
            return (4, 5, 8, 9)[i]

        def v_jobs(s, j):
            if j > 0:
                return job(s, j - 1, v_at(s, j - 1)) + 2
            if isinstance(s, int) and s == 0:
                return H + 6
            return job(s - 1, NT - 1, v_at(s - 1, NT - 1)) + 2

        def p_heads(j, i):
            return ((j - 2) * HB + i,)

        def sequences(eng, run):
            run(0, 0, False)
            run(1, 1, False)
            with eng.Fori(1, NSEQ // 2 - 1) as i:
                run(i * 2, 0, False)
                run(i * 2 + 1, 1, False)
            run(NSEQ - 2, 0, False)
            run(NSEQ - 1, 1, True)

        SPLIT_JOBS = (1, 2, 3, 4, 5, 6, 9, 10)
        SETUP = [BK[0][:, :], BK[1][:, :], SC[:, 0:BANK], SC[:, BANK:2 * BANK]]

        def split_dst(n, hi):
            cols = {1: 0, 2: BANK, 3: HW, 4: HW + BANK, 9: 2 * HW, 10: 2 * HW + BANK}
            if n in cols:
                t, c = (w_hi if hi else w_lo), cols[n]
            else:
                t, c = (a_hi if hi else a_lo), (n - 5) * BANK
            return t[:, c:c + BANK]

        @block.sync
        def _(sp):
            sp.dma_start(xs[0][:, :, :], x[0].rearrange("(j p) d -> p j d", p=P)).then_inc(x_in[0], 16)
            sp.dma_start(wg_in[:, :], Wg).then_inc(small_loaded, 16)
            for n, w in enumerate((Wr, Wkf, Wvf)):
                sp.dma_start(ffn_in[:, n, :], w).then_inc(small_loaded, 16)
            sp.dma_start(bg_all[:, :], bg.partition_broadcast(P)).then_inc(small_loaded, 16)
            sp.dma_start(wq_in, Wq.rearrange("(h e) c -> e h c", h=H)).then_inc(wq_loaded, 16)
            sp.dma_start(wk_in, Wk.rearrange("(h e) c -> e h c", h=H)).then_inc(wk_loaded, 16)
            sp.dma_start(gain_all[:, :], gain.partition_broadcast(P)).then_inc(small_loaded, 16)
            sp.dma_start(mu[:, 0:1], mu_r.rearrange("(p o) -> p o", o=1)).then_inc(small_loaded, 16)
            sp.dma_start(mu[:, 1:2], mu_k.rearrange("(p o) -> p o", o=1)).then_inc(small_loaded, 16)
            sp.dma_start(wo_in[:, :], Wo).then_inc(wo_loaded, 16)
            sp.dma_start(wv_in[:, :, :], Wv.rearrange("(h e) c -> e h c", h=H)).then_inc(wv_loaded, 16)
            sp.dma_start(xs[1][:, :, :], x[1].rearrange("(j p) d -> p j d", p=P)).then_inc(x_in[1], 16)

            def run(s, par, last):
                known = isinstance(s, int)
                if not (known and s + 2 >= NSEQ):
                    sp.wait_ge(xn_ready, s + 1)
                    sp.dma_start(xs[par][:, :, :], x[s + 2].rearrange("(j p) d -> p j d", p=P))\
                        .then_inc(x_in[par], 16)
                if not (known and s == 0):
                    sp.wait_ge(y_ready, s)
                    sp.dma_start(out[s - 1].rearrange("(j p) d -> p j d", p=P), y[:, :, :]).then_inc(y_out, 16)
                    sp.wait_ge(y_out, s * 16)
                sp.dma_start(y[:, :, :], x[s].rearrange("(j p) d -> p j d", p=P)).then_inc(residual_in, 16)

            sequences(sp, run)
            sp.wait_ge(y_ready, NSEQ)
            sp.dma_start(out[NSEQ - 1].rearrange("(j p) d -> p j d", p=P), y[:, :, :]).then_inc(y_out, 16)
            sp.wait_ge(y_out, 16 * NSEQ)

        V_BEFORE_EXP = (0, 3)
        DVE_MASKS = (1, 2, 3)
        PE_MASKS = tuple(j for j in range(NT) if j not in DVE_MASKS)
        NSMALL = 16 * 8

        @block.tensor
        def _(pe):
            def setup_job(n):
                need(pe, setup_read, n - 3)
                pb = SETUP[n % 4]
                if n == 0:
                    for i in range(3):
                        pe.transpose(pb[:, i * D:(i + 1) * D], ffn_in[:, i, :], ident[:, :])
                    last = pe.transpose(pb[:, 3 * D:3 * D + H], wg_in[:, :], ident[0:H, 0:H])
                elif n < 5:
                    w = (wq_in, wk_in)[(n - 1) // 2]
                    for i in range(HB):
                        last = pe.transpose(pb[:, i * D:(i + 1) * D], w[:, (n - 1) % 2 * HB + i, :], ident[:, :])
                elif n < 7:
                    for i in range(HB):
                        h = (n - 5) * HB + i
                        last = pe.matmul(pb[:, i * D:(i + 1) * D], wq_in[:, h, :], wk_in[:, h, :],
                                         start=True, stop=True)
                elif n < 9:
                    for i in range(HB):
                        h = (n - 7) * HB + i
                        last = pe.transpose(pb[:, i * D:(i + 1) * D], wo_in[:, h * D:(h + 1) * D], ident[:, :])
                else:
                    pe.wait_ge(setup_read, n - 1)
                    for i in range(HB):
                        h = (n - 9) * HB + i
                        last = pe.matmul(pb[:, i * D:(i + 1) * D], wv_in[:, h, :], woT[:, h, :],
                                         start=True, stop=True)
                last.then_inc(setup_filled, 1)

            def xT_stage(s, par):
                pe.wait_ge(xn_ready, s + 1)
                for j in range(NT):
                    last = pe.transpose(MI[:, j * P:(j + 1) * P], xn[par][:, j, :], ident[:, :])
                last.then_inc(xT_filled, 1)

            def z_stage(s, par):
                pe.wait_ge(xhi_ready, s + 1)
                for j in range(NT):
                    last = pe.matmul(MI[:, j * H:(j + 1) * H], xT[par][:, 1 + j * P:1 + (j + 1) * P],
                                     small_wT[:, 3 * D:3 * D + H], start=True, stop=True)
                last.then_inc(z_filled, 1)

            def gate_stage(s):
                pe.wait_ge(logg_ready, s + 1)
                for kind in range(3):
                    last = pe.matmul(MI[:, kind * NT * H:(kind + 1) * NT * H], span[:, kind, :],
                                     log_g[:, :, :].rearrange("p j h -> p (j h)"), start=True, stop=True)
                last.then_inc(gates_filled, 1)

            def r_stage(s):
                pe.wait_ge(xrk_ready, s + 1)
                pe.matmul(MI[:, :], small_wT[:, 0:D], xr[:, :], start=True, stop=True).then_inc(r_filled, 1)

            def k_stage(s):
                pe.wait_ge(rexp_ready, s + 1)
                pe.matmul(MI[:, :], small_wT[:, D:2 * D], xk[:, :], start=True, stop=True).then_inc(k_filled, 1)

            def v_stage(s):
                pe.wait_ge(kact_ready, s + 1)
                pe.wait_ge(partsT_ready, s * NT + 2)
                pe.matmul(MI[:, :], small_wT[:, 2 * D:3 * D], k_act[:, :], start=True, stop=True)\
                    .then_inc(v_filled, 1)

            def product(n, pb, hi_lo_pairs):
                need(pe, proj_read, n - 1)
                for i, (lhsT, rhs) in enumerate(hi_lo_pairs):
                    last = pe.matmul(pb[:, :], lhsT, rhs, start=(i == 0), stop=(i == len(hi_lo_pairs) - 1))
                last.then_inc(proj_filled, 1)

            def p_stage(s, par, hs, first_job):
                pe.wait_ge(xlo_ready, s + 1)
                for i, h in enumerate(hs):
                    cols = slice(h * D, (h + 1) * D)
                    product(first_job + i, PJ[h % 2], [(a_hi[:, cols], xT_hi[par][:, :]),
                                                       (a_hi[:, cols], xT_lo[par][:, :]),
                                                       (a_lo[:, cols], xT_hi[par][:, :])])

            def project(par, j, first_job, ks):
                t = slice(j * P, (j + 1) * P)
                for i, k in enumerate(ks):
                    cols = slice(k * BANK, (k + 1) * BANK)
                    product(first_job + i, PJ[k % 2], [(xT_hi[par][:, t], w_hi[:, cols]),
                                                       (xT_hi[par][:, t], w_lo[:, cols]),
                                                       (xT_lo[par][:, t], w_hi[:, cols])])

            def spread(dst, j0, b):
                for i in range(HB):
                    last = pe.matmul(dst[:, i * P:(i + 1) * P], pick[:, j0 + i, :], partsT[b % 2][:, :],
                                     start=True, stop=True)
                return last

            def turn(b, g):
                pe.wait_ge(att_a_ready, g + 1)
                pe.wait_ge(att_b_ready, g + 1)
                for half in range(2):
                    for h in range(half * HB, (half + 1) * HB):
                        last = pe.transpose(SC[:, h * P:(h + 1) * P], att[b][:, h, :], ident[:, :])
                    last.then_inc(attT_filled, 1)

            def attend(s, par, j):
                g = s * NT + j
                pe.wait_ge(proj_read, v_jobs(s, j))
                if j == 0:
                    need(pe, y_ready, s)
                for h in range(H):
                    if h % HB == 0:
                        pe.wait_ge(attT_ready, g * 2 + 1 + h // HB)
                    last = pe.matmul(OUT[:, j * P:(j + 1) * P], vp[j % 2][:, h * D:(h + 1) * D],
                                     attT[j % 2][:, h, :], start=(j == 0 and h == 0), stop=(h == H - 1))
                last.then_inc(av_done, 1)

            def cross(s, j, half):
                pe.wait_ge(pdec_ready, s * 6 + 2 * (j - 1) + half + 1)
                for h in range(half * HB, (half + 1) * HB):
                    last = pe.matmul(OUT[:, j * P:(j + 1) * P], state[:, h, :], p_dec[:, h, :],
                                     start=(h == 0), stop=False)
                if half == 1:
                    last.then_inc(cross_done, 1)

            def increment(s, j, half):
                if j == 0:
                    pe.wait_ge(xnlo_ready, s + 1)
                pe.wait_ge(vlo_ready, s * 6 + 2 * j + half + 1)
                cols = slice(half * BANK, (half + 1) * BANK)
                pe.matmul(BK[half][:, :], xn_hi[:, j, :], v_hi[:, cols], start=True, stop=False)
                pe.matmul(BK[half][:, :], xn_hi[:, j, :], v_lo[:, cols], start=False, stop=False)
                pe.matmul(BK[half][:, :], xn_lo[:, j, :], v_hi[:, cols], start=False, stop=True)\
                    .then_inc(incr_filled, 1)

            def finish(s):
                pe.wait_ge(sg_ready, s + 1)
                for j in range(NT):
                    last = pe.transpose(OUT[:, j * P:(j + 1) * P], sgT[:, j * P:(j + 1) * P], ident[:, :])
                last.then_inc(outT_filled, 1)

            pe.wait_ge(ident_ready, 2)
            xT_stage(0, 0)
            pe.wait_ge(small_loaded, NSMALL)
            setup_job(0)
            pe.wait_ge(wq_loaded, 16)
            setup_job(1)
            setup_job(2)
            pe.wait_ge(wk_loaded, 16)
            pe.wait_ge(setup_read, 1)
            z_stage(0, 0)
            setup_job(3)
            setup_job(4)
            pe.wait_ge(consts_ready, 1)
            gate_stage(0)
            setup_job(5)
            setup_job(6)
            pe.wait_ge(xlo_ready, 1)
            pe.wait_ge(setup_read, 5)
            project(0, 0, 0, range(4))
            pe.wait_ge(wo_loaded, 16)
            setup_job(7)
            setup_job(8)
            pe.wait_ge(wv_loaded, 16)
            pe.wait_ge(setup_read, 7)
            p_stage(0, 0, (0, 1), 4)
            setup_job(9)
            p_stage(0, 0, (2, 3), 6)
            setup_job(10)
            p_stage(0, 0, range(HB, H), 8)
            pe.wait_ge(setup_read, 11)
            project(0, 0, H + 4, (4, 5))
            pe.wait_ge(pick_ready, 7)

            def run(s, par, last_s):
                for j in range(NT):
                    g = s * NT + j
                    nxt = not (last_s and j == NT - 1)
                    np_, nj = (par, j + 1) if j < NT - 1 else (1 - par, 0)
                    if nxt:
                        if j == NT - 1:
                            pe.wait_ge(xlo_ready, s + 2)
                        project(np_, nj, job(s, j, 0), (0,))
                    pe.wait_ge(parts_ready, g + 1)
                    if isinstance(s, int) and s == 0 and j == 0:
                        pe.wait_ge(decay_ready, 1)
                    elif j == 1:
                        pe.wait_ge(krelu_ready, s + 1)
                    elif j == 2:
                        if last_s:
                            pe.wait_ge(ffn_ready, s + 1)
                        else:
                            pe.wait_ge(xhi_ready, s + 2)
                    elif j == 3 and not last_s:
                        pe.wait_ge(decay_ready, s + 2)
                    else:
                        pe.wait_ge(partsT_ready, g)
                    pe.transpose(MI16[:, 0:P], parts[:, :], ident16[:, :]).then_inc(partsT_filled, 1)
                    if nxt:
                        project(np_, nj, job(s, j, 1), (1,))
                    if not (isinstance(s, int) and s == 0 and j == 0):
                        turn((j + 1) % 2, g - 1)
                    pe.wait_ge(partsT_ready, g + 1)
                    for half in range(2):
                        if j > 0:
                            pe.wait_ge(state_ready, s * 6 + 2 * j - 1 + half)
                        spread(BK[half][:, :], half * HB, j).then_inc(qrms_filled, 1)
                    if j > 0:
                        attend(s, par, j - 1)
                    elif not (isinstance(s, int) and s == 0):
                        attend(s - 1, 1 - par, NT - 1)
                    for half in range(2):
                        spread(SC[:, half * BANK:(half + 1) * BANK], H + half * HB, j).then_inc(krms_filled, 1)
                    if j == 1:
                        v_stage(s)
                    if nxt:
                        project(np_, nj, job(s, j, 2), (2,))
                    if j == 2 and not last_s:
                        z_stage(s + 1, 1 - par)
                    if nxt:
                        project(np_, nj, job(s, j, 3), (3,))
                    for half in range(2):
                        pe.wait_ge(krms_ready, g * 2 + half + 1)
                        if j in PE_MASKS:
                            pe.matmul(SC[:, half * BANK:(half + 1) * BANK], ident16[:, :],
                                      mask16[:, :, :].rearrange("p h s -> p (h s)"), start=True, stop=False)
                    for half in range(2):
                        pe.wait_ge(pq_ready, g * 2 + half + 1)
                        for h in range(half * HB, (half + 1) * HB):
                            last = pe.matmul(SC[:, h * P:(h + 1) * P], p_q[j % 2][:, h, :],
                                             xT[par][:, 1 + j * P:1 + (j + 1) * P], start=(j not in PE_MASKS),
                                             stop=(j not in PE_MASKS or h % HB == HB - 1))
                        last.then_inc(scores_filled, 1)
                    makes_p = j >= 2 and not last_s
                    if j == 0:
                        pe.wait_ge(partsT_ready, g + 1)
                        r_stage(s)
                        if not (isinstance(s, int) and s == 0):
                            finish(s - 1)
                    if j == 1 and not last_s:
                        pe.wait_ge(ffn_ready, s + 1)
                        xT_stage(s + 1, 1 - par)
                    for half in range(2):
                        if makes_p:
                            p_stage(s + 1, 1 - par, p_heads(j, half), job(s, j, p_at(half)))
                        if j == NT - 1 and half == 1 and nxt:
                            project(np_, nj, job(s, j, v_at(s, j)), (4,))
                        if j > 0:
                            cross(s, j, half)
                    for half in range(2):
                        if nxt and not (j == NT - 1 and half == 0):
                            project(np_, nj, job(s, j, v_at(s, j) + half), (4 + half,))
                        if j < NT - 1:
                            increment(s, j, half)
                        if j == 0 and half == 0:
                            k_stage(s)
                    if makes_p:
                        p_stage(s + 1, 1 - par, p_heads(j, 2), job(s, j, p_at(2)))
                        if j == 2:
                            gate_stage(s + 1)
                        p_stage(s + 1, 1 - par, p_heads(j, 3), job(s, j, p_at(3)))

            sequences(pe, run)
            turn(1, NSEQ * NT - 1)
            attend(NSEQ - 1, 1, NT - 1)
            finish(NSEQ - 1)

        @block.scalar
        def _(act):
            def setup_hi_stage(n):
                act.wait_ge(setup_filled, n + 1)
                act.activation(split_dst(n, True), SETUP[n % 4], ACT.Copy).then_inc(setup_hi, 1)

            def norm_stage(s):
                act.wait_ge(var_ready, s + 1)
                act.activation(ln_var[:, :], mean_var[:, :, 1], ACT.Ln, bias=eps[:, 0:1]).then_inc(lnvar_done, 1)
                act.wait_ge(lnvar_done, s + 1)
                act.activation(rstd[:, :], ln_var[:, :], ACT.Exp, scale=-0.5).then_inc(rstd_ready, 1)

            def xT_stage(s, par):
                act.wait_ge(xT_filled, s + 1)
                act.activation(xT[par][:, 1:1 + T], MI[:, :], ACT.Copy).then_inc(xT_ready, 1)
                act.activation(xT_hi[par][:, :], MI[:, :], ACT.Copy).then_inc(xhi_ready, 1)

            def xn_hi_stage(s, par):
                act.wait_ge(xn_ready, s + 1)
                need(act, incr_filled, s * 6)
                act.activation(xn_hi[:, :, :], xn[par][:, :, :], ACT.Copy).then_inc(xnhi_ready, 1)

            def v_hi_stage(s, j):
                for half in range(2):
                    act.wait_ge(vscaled_ready, s * 6 + 2 * j + half + 1)
                    cols = slice(half * BANK, (half + 1) * BANK)
                    act.activation(v_hi[:, cols], v_scaled[:, cols], ACT.Copy).then_inc(vhi_ready, 1)

            def mix_stage(s, par):
                act.wait_ge(xT_ready, s + 1)
                if isinstance(s, int) and s == 0:
                    act.wait_ge(small_ready, 2)
                need(act, xrk_ready, s)
                act.activation(mix_r[:, :], xT[par][:, 0:T], ACT.Copy, scale=one_minus_mu[:, 0:1]).then_inc(mix_ready, 1)
                act.activation(mix_k[:, :], xT[par][:, 0:T], ACT.Copy, scale=one_minus_mu[:, 1:2]).then_inc(mix_ready, 1)

            def gate_log_stage(s):
                act.wait_ge(zneg_ready, s + 1)
                act.activation(z_l1p[:, :, :], z_neg[:, :, :], ACT.Exp).then_inc(zexp_done, 1)
                act.wait_ge(zexp_done, s + 1)
                act.activation(z_l1p[:, :, :], z_l1p[:, :, :], ACT.Ln, bias=1.0).then_inc(zl1p_ready, 1)

            def decay_stage(s, par):
                act.wait_ge(gates_filled, s + 1)
                n = NT * H
                act.activation(q_decay[par][:, :, :, 1], MI[:, 0:n].rearrange("p (j h) -> p j h", j=NT), ACT.Exp)
                act.activation(decay[par][:, :, :, :].rearrange("p k j h -> p (k j h)"), MI[:, n:3 * n], ACT.Exp)\
                    .then_inc(decay_ready, 1)

            def r_stage(s):
                act.wait_ge(r_filled, s + 1)
                need(act, rone_done, s)
                act.activation(r_exp[:, :], MI[:, :], ACT.Exp, scale=-1.0).then_inc(rexp_ready, 1)

            def k_stage(s):
                act.wait_ge(k_filled, s + 1)
                act.activation(k_relu[:, :], MI[:, :], ACT.Relu).then_inc(krelu_ready, 1)
                act.wait_ge(krelu_ready, s + 1)
                need(act, v_filled, s)
                act.activation(k_act[:, :], k_relu[:, :], ACT.Square).then_inc(kact_ready, 1)

            def f_stage(s):
                act.wait_ge(ffn_ready, s + 1)
                act.activation(f_exp[:, :], ffn[:, :], ACT.Exp, scale=-1.0).then_inc(fexp_ready, 1)

            def p_stage(s, par, hs, first_job):
                for i, h in enumerate(hs):
                    act.wait_ge(proj_filled, first_job + i + 1)
                    act.activation(p_raw[par][:, h, :], PJ[h % 2][:, :], ACT.Copy).then_inc(proj_read, 1)

            def squares(b, first_job, k):
                act.wait_ge(proj_filled, first_job + k + 1)
                for i in range(HB):
                    last = act.activation(squared[:, k * HB + i, :], PJ[k % 2][:, i * D:(i + 1) * D], ACT.Square,
                                          accum_out=ssq[b][:, k * HB + i:k * HB + i + 1])
                last.then_inc(proj_read, 1)

            def rms_stage(b, first_job, count):
                act.wait_ge(proj_read, first_job + 4)
                act.activation(ln_ms[:, :], ssq[b][:, :], ACT.Ln, bias=eps[:, 1:2], scale=1.0 / DK)\
                    .then_inc(lnms_done, 1)
                act.wait_ge(lnms_done, count)
                act.activation(rms[b][:, :], ln_ms[:, :], ACT.Exp, scale=-0.5).then_inc(rms_ready, 1)

            def v_stage(b, first_job, i, tiles_done):
                need(act, av_done, tiles_done)
                act.wait_ge(proj_filled, first_job + i + 1)
                act.activation(vp[b][:, i * BANK:(i + 1) * BANK], PJ[i][:, :], ACT.Copy).then_inc(proj_read, 1)

            act.preload_act_table_set("natural_log_exp_and_others")
            act.wait_ge(small_ready, 1)
            norm_stage(0)
            xT_stage(0, 0)
            xn_hi_stage(0, 0)
            for n in range(1, 3):
                setup_hi_stage(n)
            gate_log_stage(0)
            setup_hi_stage(3)
            mix_stage(0, 0)
            setup_hi_stage(4)
            decay_stage(0, 0)
            setup_hi_stage(5)
            setup_hi_stage(6)
            for k in range(4):
                squares(0, 0, k)
            rms_stage(0, 0, 1)
            p_stage(0, 0, (0, 1), 4)
            setup_hi_stage(9)
            p_stage(0, 0, (2, 3), 6)
            setup_hi_stage(10)
            p_stage(0, 0, range(HB, H), 8)
            for i in range(2):
                v_stage(0, H + 4, i, 0)

            def attT_stage(b, g):
                for half in range(2):
                    act.wait_ge(attT_filled, g * 2 + half + 1)
                    act.activation(attT[b][:, half * HB:(half + 1) * HB, :],
                                   SCh[:, half * HB:(half + 1) * HB, :], ACT.Copy).then_inc(attT_ready, 1)

            def run(s, par, last_s):
                for j in range(NT):
                    g = s * NT + j
                    nxt = not (last_s and j == NT - 1)
                    nb = (j + 1) % 2
                    if nxt:
                        squares(nb, job(s, j, 0), 0)
                    if not (isinstance(s, int) and s == 0 and j == 0):
                        attT_stage(nb, g - 1)
                    if nxt:
                        squares(nb, job(s, j, 0), 1)
                    if j < NT - 1:
                        v_hi_stage(s, j)
                    elif not last_s:
                        xn_hi_stage(s + 1, 1 - par)
                    for half in range(2):
                        act.wait_ge(krms_filled, g * 2 + half + 1)
                        act.activation(k_rms[j % 2][:, half * BANK:(half + 1) * BANK],
                                       SC[:, half * BANK:(half + 1) * BANK], ACT.Copy).then_inc(krms_ready, 1)
                    if nxt:
                        squares(nb, job(s, j, 0), 2)
                    if j == 0 and not last_s:
                        norm_stage(s + 1)
                    if j == 2 and not last_s:
                        mix_stage(s + 1, 1 - par)
                    if nxt:
                        squares(nb, job(s, j, 0), 3)
                    if j == 2 and not last_s:
                        gate_log_stage(s + 1)
                    if nxt:
                        rms_stage(nb, job(s, j, 0), g + 2)
                    makes_p = j >= 2 and not last_s
                    if j == 0:
                        r_stage(s)
                    if j == 1 and not last_s:
                        xT_stage(s + 1, 1 - par)
                    if makes_p:
                        for i in range(2):
                            p_stage(s + 1, 1 - par, p_heads(j, i), job(s, j, p_at(i)))
                    if j in V_BEFORE_EXP and nxt:
                        v_stage(nb, job(s, j, v_at(s, j)), 0, g)
                    act.wait_ge(shifted_ready, g + 1)
                    act.activation(own[j % 2][:, :, :], own[j % 2][:, :, :], ACT.Exp, scale=SCALE)\
                        .then_inc(exp_ready, 1)
                    if j == 0:
                        k_stage(s)
                    if nxt:
                        for i in range(1 if j in V_BEFORE_EXP else 0, 2):
                            v_stage(nb, job(s, j, v_at(s, j)), i, g)
                    if j == 1:
                        f_stage(s)
                    if makes_p:
                        p_stage(s + 1, 1 - par, p_heads(j, 2), job(s, j, p_at(2)))
                        if j == 2:
                            decay_stage(s + 1, 1 - par)
                        p_stage(s + 1, 1 - par, p_heads(j, 3), job(s, j, p_at(3)))

            sequences(act, run)
            attT_stage(1, NSEQ * NT - 1)

        @block.vector
        def _(dve):
            dve.memset(eps[:, 0:1], LN_EPS)
            dve.memset(eps[:, 1:2], RMS_EPS).then_inc(small_ready, 1)
            for b in range(2):
                dve.memset(xT[b][:, 0:1], 0.0)

            def norm_stats(s, par, loads):
                dve.wait_ge(x_in[par], loads)
                for j in range(NT):
                    last = dve.bn_stats(stats[:, j, :], xs[par][:, j, :])
                last.then_inc(stats_done, 1)
                dve.wait_ge(stats_done, s + 1)
                dve.memset(scratch[:, :], 0.0)
                for j in range(NT):
                    last = dve.bn_aggr(mean_var[:, j, :], stats[:, j, :])
                last.then_inc(var_ready, 1)

            def norm_stage(s, par):
                dve.wait_ge(var_ready, s + 1)
                dve.wait_ge(rstd_ready, s + 1)
                for j in range(NT):
                    last = dve.tensor_scalar(xn[par][:, j, :], xs[par][:, j, :], mean_var[:, j, 0:1],
                                             rstd[:, j:j + 1], ALU.subtract, ALU.mult)
                last.then_inc(xn_ready, 1)

            def xlo_stage(s, par):
                dve.wait_ge(xhi_ready, s + 1)
                dve.tensor_tensor(xT_lo[par][:, :], xT[par][:, 1:1 + T], xT_hi[par][:, :].bitcast(F32),
                                  ALU.subtract).then_inc(xlo_ready, 1)

            def mix_stage(s, par):
                dve.wait_ge(mix_ready, s * 2 + 2)
                need(dve, k_filled, s)
                dve.scalar_tensor_tensor(xr[:, :], xT[par][:, 1:1 + T], mu[:, 0:1], mix_r[:, :], ALU.mult, ALU.add)
                dve.scalar_tensor_tensor(xk[:, :], xT[par][:, 1:1 + T], mu[:, 1:2], mix_k[:, :], ALU.mult, ALU.add)\
                    .then_inc(xrk_ready, 1)

            def z_stage(s):
                dve.wait_ge(z_filled, s + 1)
                dve.tensor_tensor(zb[:, :, :], MI[:, 0:NT * H].rearrange("p (j h) -> p j h", j=NT),
                                  bg_all[:, :].rearrange("p (o h) -> p o h", o=1).broadcast_to([P, NT, H]), ALU.add)\
                    .then_inc(zb_done, 1)
                dve.wait_ge(zb_done, s + 1)
                dve.scalar_tensor_tensor(z_neg[:, :, :], zb[:, :, :], -1.0, zb[:, :, :], ALU.mult, ALU.min)\
                    .then_inc(zneg_ready, 1)

            def gate_stage(s):
                dve.wait_ge(zl1p_ready, s + 1)
                dve.scalar_tensor_tensor(log_g[:, :, :], zb[:, :, :], 0.0, z_l1p[:, :, :], ALU.min, ALU.subtract)\
                    .then_inc(logg_ready, 1)

            HALF = T // 2

            def r_stage(s, half):
                dve.wait_ge(rone_done, s + 1)
                t = slice(half * HALF, (half + 1) * HALF)
                dve.reciprocal(r_sig[:, t], r_sig[:, t]).then_inc(rsig_done, 1)

            def v_stage(s):
                dve.wait_ge(v_filled, s + 1)
                dve.wait_ge(rsig_done, s * 2 + 2)
                dve.tensor_tensor(ffn[:, :], MI[:, :], r_sig[:, :], ALU.mult).then_inc(ffn_ready, 1)

            def f_stage(s, half):
                if half == 0:
                    dve.wait_ge(fexp_ready, s + 1)
                    dve.tensor_scalar(f_exp[:, :], f_exp[:, :], 1.0, None, ALU.add).then_inc(fone_done, 1)
                    dve.wait_ge(fone_done, s + 1)
                t = slice(half * HALF, (half + 1) * HALF)
                dve.reciprocal(f_exp[:, t], f_exp[:, t]).then_inc(fsig_done, 1)

            def silu_stage(s, par):
                dve.wait_ge(fsig_done, s * 2 + 2)
                dve.tensor_tensor(gT[par][:, :], ffn[:, :], f_exp[:, :], ALU.mult).then_inc(gT_ready, 1)

            def split_factors(step, b, count):
                if step == 0:
                    dve.wait_ge(rms_ready, count)
                    dve.tensor_scalar(rms[b][:, 0:H], rms[b][:, 0:H], gain_all[:, 0:1], None, ALU.mult)\
                        .then_inc(gained, 1)
                elif step == 1:
                    dve.wait_ge(gained, count)
                    need(dve, partsT_filled, count - 1)
                    dve.tensor_copy(parts[:, 0:NR], rms[b][:, :]).then_inc(split_step, 1)
                elif step == 2:
                    dve.wait_ge(split_step, count * 4 - 3)
                    dve.tensor_tensor(res1[:, :], rms[b][:, :], parts[:, 0:NR], ALU.subtract).then_inc(split_step, 1)
                elif step == 3:
                    dve.wait_ge(split_step, count * 4 - 2)
                    dve.tensor_copy(parts[:, NR:2 * NR], res1[:, :]).then_inc(split_step, 1)
                elif step == 4:
                    dve.wait_ge(split_step, count * 4 - 1)
                    dve.tensor_tensor(res2[:, :], res1[:, :], parts[:, NR:2 * NR], ALU.subtract)\
                        .then_inc(split_step, 1)
                else:
                    dve.wait_ge(split_step, count * 4)
                    dve.tensor_copy(parts[:, 2 * NR:3 * NR], res2[:, :]).then_inc(parts_ready, 1)

            def setup_stage(n):
                dve.wait_ge(setup_filled, n + 1)
                if n in SPLIT_JOBS:
                    dve.wait_ge(setup_hi, SPLIT_JOBS.index(n) + 1)
                    last = dve.tensor_tensor(split_dst(n, False), SETUP[n % 4], split_dst(n, True).bitcast(F32),
                                             ALU.subtract)
                elif n == 0:
                    last = dve.tensor_copy(small_wT[:, :], SETUP[n % 4][:, 0:3 * D + H])
                else:
                    last = dve.tensor_copy(woT[:, (n - 7) * HB:(n - 6) * HB, :].rearrange("p h d -> p (h d)"),
                                           SETUP[n % 4])
                last.then_inc(setup_read, 1)

            def partsT_stage(b, count):
                dve.wait_ge(partsT_filled, count)
                dve.tensor_copy(partsT[b][:, :], MI16[:, 0:P]).then_inc(partsT_ready, 1)

            def state_update(s, j, half):
                dve.wait_ge(incr_filled, s * 6 + 2 * j + half + 1)
                part = state[:, half * HB:(half + 1) * HB, :].rearrange("p h d -> p (h d)")
                if j == 0:
                    last = dve.tensor_copy(part, BK[half][:, :])
                else:
                    dve.wait_ge(state_decayed, s * 4 + 2 * (j - 1) + half + 1)
                    last = dve.tensor_tensor(part, part, BK[half][:, :], ALU.add)
                last.then_inc(state_ready, 1)

            y_flat = y[:, :, :].rearrange("p j d -> p (j d)")
            norm_stats(0, 0, 16)
            norm_stage(0, 0)
            dve.memset(span[:, :, :], 0.0).then_inc(zeroed, 1)
            dve.memset(parts[:, :], 0.0)
            for b in range(2):
                dve.memset(q_decay[b][:, :, :, 0], 1.0)
            dve.wait_ge(zeroed, 1)
            dve.memset(span[0:CH, 0, :], 1.0)
            dve.memset(span[:, 1, :], 1.0)
            dve.memset(span[CH:P, 2, 0:CH], 1.0).then_inc(consts_ready, 1)
            for b in range(2):
                dve.memset(att[b][:, :, :], 0.0)
            setup_stage(0)
            xlo_stage(0, 0)
            setup_stage(1)
            setup_stage(2)
            dve.wait_ge(small_loaded, NSMALL)
            dve.tensor_scalar(one_minus_mu[:, :], mu[:, :], -1.0, 1.0, ALU.mult, ALU.add).then_inc(small_ready, 1)
            z_stage(0)
            setup_stage(3)
            gate_stage(0)
            setup_stage(4)
            mix_stage(0, 0)
            for n in range(5, 9):
                setup_stage(n)
            for step in range(6):
                split_factors(step, 0, 1)
            setup_stage(9)
            setup_stage(10)
            partsT_stage(0, 1)

            def run(s, par, last_s):
                first = isinstance(s, int) and s == 0
                for j in range(NT):
                    g = s * NT + j
                    b = j % 2
                    nxt = not (last_s and j == NT - 1)
                    if j == 0:
                        dve.wait_ge(proj_read, H + 4 if first else job(s - 1, NT - 1, p_at(3)) + 1)
                    for half in range(2):
                        dve.wait_ge(qrms_filled, g * 2 + half + 1)
                        hs = slice(half * HB, (half + 1) * HB)
                        dve.tensor_tensor(p_q[b][:, hs, :], p_raw[par][:, hs, j * P:(j + 1) * P],
                                          BK[half][:, :].rearrange("p (h t) -> p h t", h=HB), ALU.mult)\
                            .then_inc(pq_ready, 1)
                    if j == 0 and not first:
                        dve.wait_ge(av_done, g)
                        dve.wait_ge(gT_ready, s)
                        dve.tensor_tensor(sgT[:, :], OUT[:, :], gT[1 - par][:, :], ALU.mult).then_inc(sg_ready, 1)
                    if j == 0:
                        if not last_s:
                            norm_stats(s + 1, 1 - par, x_loads(s, par))
                    if j == 1:
                        if not last_s:
                            norm_stage(s + 1, 1 - par)
                        r_stage(s, 1)
                        v_stage(s)
                    if j == 2:
                        if not last_s:
                            xlo_stage(s + 1, 1 - par)
                            z_stage(s + 1)
                        f_stage(s, 0)
                    if j == 3:
                        if not last_s:
                            mix_stage(s + 1, 1 - par)
                        f_stage(s, 1)
                    kr = k_rms[b][:, :].rearrange("p (h s) -> p h s", h=H)
                    for half in range(2):
                        dve.wait_ge(krms_ready, g * 2 + half + 1)
                        dve.wait_ge(scores_filled, g * 2 + half + 1)
                        hs = slice(half * HB, (half + 1) * HB)
                        dve.tensor_tensor(own[b][0:CH, hs, :], SCh[0:CH, hs, 0:CH], kr[0:CH, hs, 0:CH], ALU.mult)
                        last = dve.tensor_tensor(own[b][CH:P, hs, :], SCh[CH:P, hs, CH:P], kr[CH:P, hs, CH:P],
                                                 ALU.mult)
                    last.then_inc(own_ready, 1)
                    if nxt:
                        split_factors(0, (j + 1) % 2, g + 2)
                    dve.wait_ge(own_ready, g + 1)
                    if j in DVE_MASKS:
                        dve.tensor_tensor(own[b][:, :, :], own[b][:, :, :],
                                          mask[:, :].rearrange("p (o s) -> p o s", o=1).broadcast_to([P, H, CH]),
                                          ALU.add).then_inc(mask_ready, 1)
                        dve.wait_ge(mask_ready, s * len(DVE_MASKS) + DVE_MASKS.index(j) + 1)
                    dve.tensor_reduce(top[:, :], own[b][:, :, :], AX.X, ALU.max).then_inc(top_done, 1)
                    if nxt:
                        split_factors(1, (j + 1) % 2, g + 2)
                    dve.wait_ge(top_done, g + 1)
                    dve.tensor_tensor(own[b][:, :, :], own[b][:, :, :], over(top), ALU.subtract)\
                        .then_inc(shifted_ready, 1)
                    if nxt:
                        split_factors(2, (j + 1) % 2, g + 2)
                    dve.tensor_tensor(att[b][CH:P, :, 0:CH], SCh[CH:P, :, 0:CH], kr[CH:P, :, 0:CH], ALU.mult)
                    if j == 2 and not last_s:
                        gate_stage(s + 1)
                    if nxt:
                        split_factors(3, (j + 1) % 2, g + 2)
                    if nxt:
                        split_factors(4, (j + 1) % 2, g + 2)
                    dve.wait_ge(exp_ready, g + 1)
                    dve.tensor_reduce(total[:, :], own[b][:, :, :], AX.X, ALU.add).then_inc(total_done, 1)
                    if nxt:
                        split_factors(5, (j + 1) % 2, g + 2)
                    dve.wait_ge(total_done, g + 1)
                    dve.reciprocal(inv_total[b][:, :], total[:, :]).then_inc(inv_ready, 1)
                    dve.wait_ge(inv_ready, g + 1)
                    dve.tensor_tensor(att[b][0:CH, :, 0:CH], own[b][0:CH, :, :], over(inv_total[b])[0:CH, :, :],
                                      ALU.mult).then_inc(att_a_ready, 1)
                    if j < NT - 1:
                        state_update(s, j, 0)
                    if nxt:
                        partsT_stage((j + 1) % 2, g + 2)
                    if j < NT - 1:
                        state_update(s, j, 1)
                    if j == 0 and not first:
                        dve.wait_ge(outT_filled, s)
                        dve.wait_ge(residual_in, s * 16)
                        dve.tensor_tensor(y_flat, OUT[:, :], y_flat, ALU.add)\
                            .then_inc(y_ready, 1)
                    if j == 0:
                        r_stage(s, 0)
                    if j == 3:
                        silu_stage(s, par)

            def x_loads(s, par):
                return s * 8 + (16 if par == 0 else 24)

            def over(v):
                return v[:, :].rearrange("p (h o) -> p h o", o=1).broadcast_to([P, H, CH])

            sequences(dve, run)
            dve.wait_ge(av_done, NSEQ * NT)
            dve.wait_ge(gT_ready, NSEQ)
            dve.tensor_tensor(sgT[:, :], OUT[:, :], gT[1][:, :], ALU.mult).then_inc(sg_ready, 1)
            dve.wait_ge(outT_filled, NSEQ)
            dve.wait_ge(residual_in, 16 * NSEQ)
            dve.tensor_tensor(y_flat, OUT[:, :], y_flat, ALU.add).then_inc(y_ready, 1)

        @block.gpsimd
        def _(pool):
            pool.memset(ident[:, :], 0.0).then_inc(ident_ready, 1)
            pool.wait_ge(ident_ready, 1)
            pool.affine_select(out=ident[:, :], in_=ident[:, :], compare_op=ALU.not_equal, fill=1.0, base=0,
                               pattern=[[-1, P]], channel_multiplier=1).then_inc(ident_ready, 1)
            pool.memset(ones[:, :], 1.0)
            pool.memset(ident16[:, :], 0.0)
            pool.memset(mask[:, :], 0.0)
            pool.memset(mask16[:, :, :], 0.0)
            pool.memset(pick[:, :, :], 0.0).then_inc(pick_ready, 1)
            pool.wait_ge(pick_ready, 1)
            pool.affine_select(out=ident16[:, :], in_=ident16[:, :], compare_op=ALU.not_equal, fill=1.0, base=0,
                               pattern=[[-1, P]], channel_multiplier=1).then_inc(pick_ready, 1)
            for a in range(2):
                pool.wait_ge(pick_ready, 2 + a)
                rows = mask[a * CH:(a + 1) * CH, :]
                pool.affine_select(out=rows, in_=rows, compare_op=ALU.is_ge, fill=MASKED, base=0,
                                   pattern=[[-1, CH]], channel_multiplier=1)
                rows = mask16[a * CH:(a + 1) * CH, :, a * CH:(a + 1) * CH]
                pool.affine_select(out=rows, in_=rows, compare_op=ALU.is_ge, fill=MASKED, base=0,
                                   pattern=[[0, HB], [-1, CH]], channel_multiplier=1).then_inc(pick_ready, 1)
            for part in range(3):
                pool.wait_ge(pick_ready, part + 4)
                pool.affine_select(out=pick[:, :, :], in_=pick[:, :, :], compare_op=ALU.not_equal, fill=1.0,
                                   base=-part * NR, pattern=[[-1, NR], [0, P]], channel_multiplier=1)\
                    .then_inc(pick_ready, 1)

            def xn_lo_stage(s, par):
                pool.wait_ge(xnhi_ready, s + 1)
                pool.tensor_tensor(xn_lo[:, :, :], xn[par][:, :, :], xn_hi[:, :, :].bitcast(F32), ALU.subtract)\
                    .then_inc(xnlo_ready, 1)

            xn_lo_stage(0, 0)

            def run(s, par, last_s):
                for j in range(NT):
                    g = s * NT + j
                    b = j % 2
                    if j == 0:
                        pool.wait_ge(decay_ready, s + 1)
                    need(pool, att_b_ready, g)
                    if j < NT - 1:
                        pool.wait_ge(rms_ready, g + 1)
                        need(pool, incr_filled, s * 6 + 2 * j)
                        pool.tensor_tensor(v_scale[:, :], rms[b][:, H:NR], decay[par][:, 1, j, :], ALU.mult)\
                            .then_inc(vscale_done, 1)
                        pool.wait_ge(vscale_done, s * 3 + j + 1)
                        pool.wait_ge(proj_read, v_jobs(s, j))
                        for half in range(2):
                            hs = slice(half * HB, (half + 1) * HB)
                            cs = slice(half * BANK, (half + 1) * BANK)
                            pool.tensor_tensor(
                                v_scaled[:, cs].rearrange("p (h d) -> p h d", h=HB),
                                vp[b][:, cs].rearrange("p (h d) -> p h d", h=HB),
                                v_scale[:, hs].rearrange("p (h o) -> p h o", o=1).broadcast_to([P, HB, D]),
                                ALU.mult).then_inc(vscaled_ready, 1)
                    if j > 0:
                        need(pool, cross_done, s * 3 + j - 1)
                        for half in range(2):
                            pool.wait_ge(pq_ready, g * 2 + half + 1)
                            hs = slice(half * HB, (half + 1) * HB)
                            pool.tensor_tensor(
                                p_dec[:, hs, :].rearrange("p h (a t) -> p (h a) t", a=2),
                                p_q[b][:, hs, :].rearrange("p h (a t) -> p (h a) t", a=2),
                                q_decay[par][:, j, hs, :].rearrange("p h (a o) -> p (h a) o", o=1)
                                .broadcast_to([P, 2 * HB, CH]), ALU.mult).then_inc(pdec_ready, 1)
                    if j < NT - 1:
                        for half in range(2):
                            pool.wait_ge(vhi_ready, s * 6 + 2 * j + half + 1)
                            cs = slice(half * BANK, (half + 1) * BANK)
                            pool.tensor_tensor(v_lo[:, cs], v_scaled[:, cs], v_hi[:, cs].bitcast(F32), ALU.subtract)\
                                .then_inc(vlo_ready, 1)
                        if j == 0:
                            pool.wait_ge(rexp_ready, s + 1)
                            need(pool, ffn_ready, s)
                            pool.tensor_tensor(r_sig[:, :], r_exp[:, :], ones[:, :].broadcast_to([P, T]), ALU.add)\
                                .then_inc(rone_done, 1)
                            pool.wait_ge(rone_done, s + 1)
                        else:
                            pool.wait_ge(cross_done, s * 3 + j)
                            for half in range(2):
                                hs = slice(half * HB, (half + 1) * HB)
                                pool.tensor_tensor(state[:, hs, :], state[:, hs, :],
                                                   decay[par][:, 0, j, hs].rearrange("p (h o) -> p h o", o=1)
                                                   .broadcast_to([P, HB, D]), ALU.mult).then_inc(state_decayed, 1)
                            pool.wait_ge(state_decayed, s * 4 + 2 * j)
                    elif not last_s:
                        xn_lo_stage(s + 1, 1 - par)
                        pool.wait_ge(xnlo_ready, s + 2)
                    else:
                        pool.wait_ge(pdec_ready, s * 6 + 2 * j)
                    pool.wait_ge(inv_ready, g + 1)
                    pool.tensor_tensor(att[b][CH:P, :, CH:P], own[b][CH:P, :, :],
                                       inv_total[b][CH:P, :].rearrange("p (h o) -> p h o", o=1)
                                       .broadcast_to([CH, H, CH]), ALU.mult).then_inc(att_b_ready, 1)

            sequences(pool, run)


_INS = ["x", "Wq", "Wk", "Wv", "Wg", "bg", "Wo", "gain", "Wr", "Wkf", "Wvf", "mu_r", "mu_k"]


def kernel(L0_attn_x, L0_attn_Wq, L0_attn_Wk, L0_attn_Wv, L0_attn_Wg, L0_attn_bg, L0_attn_Wo, L0_attn_qk_gain,
           L0_ffn_W_r, L0_ffn_W_k, L0_ffn_W_v, L0_ffn_mu_r, L0_ffn_mu_k):
    import concourse.bacc as bacc
    from concourse.bass_utils import run_bass_kernel_spmd

    values = [L0_attn_x, L0_attn_Wq, L0_attn_Wk, L0_attn_Wv, L0_attn_Wg, L0_attn_bg, L0_attn_Wo,
              np.asarray(L0_attn_qk_gain).reshape(1), L0_ffn_W_r, L0_ffn_W_k, L0_ffn_W_v, L0_ffn_mu_r, L0_ffn_mu_k]
    nc = bacc.Bacc("TRN2", target_bir_lowering=False, num_devices=1)
    arrays, args = {}, []
    for name, value in zip(_INS, values):
        a = np.ascontiguousarray(value)
        arrays[f"in_{name}"] = a
        args.append(nc.dram_tensor(f"in_{name}", a.shape, mybir.dt.from_np(a.dtype), kind="ExternalInput").ap())
    shape = arrays["in_x"].shape
    args.append(nc.dram_tensor("out", shape, F32, kind="ExternalOutput").ap())
    build(nc, *args)
    r = run_bass_kernel_spmd(nc, [arrays], core_ids=[0])
    return r.results[0]["out"]
```
